# Optimizing a Trainium2 kernel written in Bass

```python
import numpy as np
import jax
import jax.numpy as jnp

def _softmax(x, axis=-1):
    return jax.nn.softmax(x, axis=axis)

def _gelu(x):
    return jax.nn.gelu(x, approximate=True)

def _silu(x):
    return jax.nn.silu(x)

def _sigmoid(x):
    return jax.nn.sigmoid(x)

def _layernorm(x, axis=-1, eps=1e-05):
    m = jnp.mean(x, axis=axis, keepdims=True)
    v = jnp.var(x, axis=axis, keepdims=True)
    return (x - m) / jnp.sqrt(v + eps)

def _scatter_add(tgt, idx, src, axis=0):
    return tgt.at[idx].add(src)

def _segment_sum(src, seg, n):
    return jax.ops.segment_sum(src, seg, n)
kernel_name = 'mk_adaln_ffn_d1_seqx_r8_861cbc'

def setup_inputs(seed: int=0):
    np.random.seed(seed)
    _w = jnp.asarray

    def _rec_inputs():
        import jax
        import jax.numpy as jnp
        _rk = jax.random.key(seed)
        x = -0.000125 + 0.9999 * jax.random.normal(jax.random.fold_in(_rk, 1), (8, 128, 512), jnp.float32)
        _lenS = 128 - jax.random.randint(jax.random.fold_in(_rk, 7), (8,), 0, max(1, 128 // 4) + 1, jnp.int32)
        _lenS2 = 128 - jax.random.randint(jax.random.fold_in(_rk, 8), (8,), 0, max(1, 128 // 4) + 1, jnp.int32)
        itok_B_0_23 = jax.random.randint(jax.random.fold_in(_rk, 11), (8,), 0, 24, jnp.int32)
        return (x, itok_B_0_23)
    x, itok_B_0_23 = _rec_inputs()

    def _L0_cond_setup():
        import jax, jax.numpy as jnp
        import numpy as np
        R = 16
        ALPHA = 32
        SCALING = ALPHA / R
        SLOTS = 32
        IN_F = 512
        OUT_F = 512
        B, T = (8, 128)
        key = jax.random.key(seed)
        k1, k2, k3, k4, k5, k6 = jax.random.split(key, 6)
        x = jax.random.normal(k1, (B, T, IN_F), dtype=jnp.float32)
        adapter_mapping = jax.random.randint(k2, (B,), 0, SLOTS, dtype=jnp.int32)
        W = jax.random.normal(k3, (OUT_F, IN_F), dtype=jnp.float32) * 0.02
        b = jax.random.normal(k4, (OUT_F,), dtype=jnp.float32) * 0.02
        lora_As = jax.random.normal(k5, (SLOTS, IN_F, R), dtype=jnp.float32) * 0.02
        lora_Bs = jax.random.normal(k6, (SLOTS, R, OUT_F), dtype=jnp.float32) * 0.02
        return {'x': x, 'adapter_mapping': adapter_mapping, 'W': W, 'b': b, 'lora_As': lora_As, 'lora_Bs': lora_Bs}
    _L0_cond_all = _L0_cond_setup()
    _L0_cond_in = {k: v for k, v in _L0_cond_all.items() if k in ('W', 'b', 'lora_As', 'lora_Bs')}
    del _L0_cond_all

    def _L0_ffn_setup():
        import jax, jax.numpy as jnp
        import numpy as np
        TOP_K = 2
        SCALING = 32.0 / 64.0
        key = jax.random.key(seed)
        ks = jax.random.split(key, 6)
        Bsz, S, Din, Dout, R, E = (4, 256, 512, 512, 64, 16)
        x = jax.random.normal(ks[0], (Bsz, S, Din), dtype=jnp.float32)
        base_w = jax.random.normal(ks[1], (Dout, Din), dtype=jnp.float32) * 0.02
        base_b = jax.random.normal(ks[2], (Dout,), dtype=jnp.float32) * 0.02
        A = jax.random.normal(ks[3], (R, Din), dtype=jnp.float32) * (1.0 / np.sqrt(Din))
        B = jax.random.normal(ks[4], (E, Dout, R), dtype=jnp.float32) * 0.02
        router_w = jax.random.normal(ks[5], (E, Din), dtype=jnp.float32) * 0.02
        return {'x': x, 'base_w': base_w, 'base_b': base_b, 'A': A, 'B': B, 'router_w': router_w}
    _L0_ffn_all = _L0_ffn_setup()
    _L0_ffn_in = {k: v for k, v in _L0_ffn_all.items() if k in ('base_w', 'base_b', 'A', 'B', 'router_w')}
    del _L0_ffn_all
    return {'x': x, 'itok_B_0_23': itok_B_0_23, 'L0_cond_W': _L0_cond_in['W'], 'L0_cond_b': _L0_cond_in['b'], 'L0_cond_lora_As': _L0_cond_in['lora_As'], 'L0_cond_lora_Bs': _L0_cond_in['lora_Bs'], 'L0_ffn_base_w': _L0_ffn_in['base_w'], 'L0_ffn_base_b': _L0_ffn_in['base_b'], 'L0_ffn_A': _L0_ffn_in['A'], 'L0_ffn_B': _L0_ffn_in['B'], 'L0_ffn_router_w': _L0_ffn_in['router_w']}

def reference(x, itok_B_0_23, L0_cond_W, L0_cond_b, L0_cond_lora_As, L0_cond_lora_Bs, L0_ffn_base_w, L0_ffn_base_b, L0_ffn_A, L0_ffn_B, L0_ffn_router_w):
    import jax
    import jax.numpy as jnp

    def _L0_cond_ref(x, adapter_mapping, W, b, lora_As, lora_Bs):
        import jax, jax.numpy as jnp
        import numpy as np
        R = 16
        ALPHA = 32
        SCALING = ALPHA / R
        SLOTS = 32
        IN_F = 512
        OUT_F = 512
        B, T = (8, 128)
        base_out = jnp.einsum('bti,oi->bto', x, W) + b
        A = lora_As[adapter_mapping]
        Bm = lora_Bs[adapter_mapping]
        lora_h = jnp.einsum('bti,bir->btr', x, A)
        lora_out = jnp.einsum('btr,bro->bto', lora_h, Bm)
        return base_out + lora_out * SCALING

    def _L0_ffn_ref(x, base_w, base_b, A, B, router_w):
        import jax, jax.numpy as jnp
        import numpy as np
        TOP_K = 2
        SCALING = 32.0 / 64.0
        base_out = jnp.einsum('bsi,oi->bso', x, base_w) + base_b
        res_hidden = jnp.einsum('bsi,ri->bsr', x, A)
        logits = jnp.einsum('bsi,ei->bse', x, router_w)
        probs = jax.nn.softmax(logits, axis=-1)
        topw, topi = jax.lax.top_k(probs, TOP_K)
        topw = topw / (jnp.sum(topw, axis=-1, keepdims=True) + 1e-06)
        num_experts = B.shape[0]
        combine = jnp.sum(jax.nn.one_hot(topi, num_experts, dtype=x.dtype) * topw[..., None], axis=-2)
        delta = jnp.einsum('bse,bsr,eor->bso', combine, res_hidden, B)
        return base_out + delta * SCALING
    x = x + _L0_ffn_ref(_L0_cond_ref(x, itok_B_0_23, L0_cond_W, L0_cond_b, L0_cond_lora_As, L0_cond_lora_Bs), L0_ffn_base_w, L0_ffn_base_b, L0_ffn_A, L0_ffn_B, L0_ffn_router_w)
    return x

_drawn_inputs = setup_inputs


def setup_inputs(seed=0):
    import zlib

    import numpy as np

    out = dict(_drawn_inputs(seed))
    spreads = {}
    factors = {'L0_cond_b': 5.454, 'L0_ffn_base_b': 2.906}
    for name, (base, spread) in spreads.items():
        noise = np.random.default_rng([zlib.crc32(name.encode()), seed]).standard_normal(out[name].shape)
        drawn = base * np.exp(spread * noise) if base else spread * noise
        out[name] = jnp.asarray(drawn.astype(out[name].dtype))
    for name, factor in factors.items():
        out[name] = (out[name] * factor).astype(out[name].dtype)
    return out
```

```python
from contextlib import ExitStack

import concourse.bass as bass
from concourse import mybir

F32 = mybir.dt.float32
F32R = mybir.dt.float32r
I32 = mybir.dt.int32
ALU = mybir.AluOpType
ACT = mybir.ActivationFunctionType
AX_X = mybir.AxisListType.X

P = 128
NT = 8
D = 512
KC = D // P
R = 16
RH = 64
E = 16
SMALL = RH + E
W2N = D + SMALL
MVN = R + SMALL
GN = E * RH
GC = GN // P
SLOTS = 32
AL = 2 * KC * R
LORA_SCALE = 2.0
DELTA_SCALE = 0.5
TOPW_EPS = 1e-6
BIAS_ROW = 4 * R


def adaln_ffn_kernel(nc, x_t, x_n, w_cat, tables, slots, b1, b2, experts, out):
    with ExitStack() as ctx:
        def sb(name, shape, dt=F32):
            return ctx.enter_context(nc.sbuf_tensor(name, shape, dt))

        def bank(name, shape=(P, D)):
            return ctx.enter_context(nc.psum_tensor(name, list(shape), F32))

        def sem(name):
            return ctx.enter_context(nc.semaphore(name))

        xt_raw = sb("xt_raw", [P, NT, KC * P])
        xn = sb("xn", [P, NT, D])
        w_raw_all = sb("w_raw_all", [P, KC * (D + W2N)])
        w_raw = w_raw_all[:, :].rearrange("p (k n) -> p k n", k=KC)
        lora_raw = sb("lora_raw", [P, NT, AL])
        exp_raw = sb("exp_raw", [P, GC, D])
        slot_row = sb("slot_row", [1, NT], I32)
        b1_col = sb("b1_col", [P, KC])
        b2_row = sb("b2_row", [1, D])
        w_hi_all = sb("w_hi_all", [P, KC * (D + W2N)], F32R)
        w_lo_all = sb("w_lo_all", [P, KC * (D + W2N)], F32R)
        w_hi = w_hi_all[:, :].rearrange("p (k n) -> p k n", k=KC)
        w_lo = w_lo_all[:, :].rearrange("p (k n) -> p k n", k=KC)
        lb_hi = sb("lb_hi", [P, KC, NT * R], F32R)
        lb_lo = sb("lb_lo", [P, KC, NT * R], F32R)
        p_hi = sb("p_hi", [P, KC, D], F32R)
        p_lo = sb("p_lo", [P, KC, D], F32R)
        mv_hi = sb("mv_hi", [P, 2, KC, MVN], F32R)
        mv_lo = sb("mv_lo", [P, 2, KC, MVN], F32R)
        c_hi = sb("c_hi", [P, W2N], F32R)
        c_lo = sb("c_lo", [P, W2N], F32R)
        bias_part = sb("bias_part", [P, W2N])
        bp_hi = sb("bp_hi", [P, W2N], F32R)
        bp_lo = sb("bp_lo", [P, W2N], F32R)
        bias_row = bias_part[0:1, :]
        br_hi = bp_hi[0:1, :]
        br_lo = bp_lo[0:1, :]
        c_stack = sb("c_stack", [P, NT, W2N], F32R)
        e_hi = sb("e_hi", [P, GC, D], F32R)
        e_lo = sb("e_lo", [P, GC, D], F32R)
        x_hi = sb("x_hi", [P, 2, KC, P], F32R)
        x_lo = sb("x_lo", [P, 2, KC, P], F32R)
        ident = sb("ident", [P, P])
        ones = sb("ones", [P, P], F32R)
        h_stack = sb("h_stack", [P, P])
        ht = sb("ht", [P, 2, P], F32R)
        small = sb("small", [P, SMALL])
        neg_max = sb("neg_max", [P, 1])
        probs = sb("probs", [P, E + 8])
        prob_sum = sb("prob_sum", [P, 1])
        top8 = sb("top8", [P, 8])
        chosen = sb("chosen", [P, 8])
        rest = sb("rest", [P, E + 8])
        picked = sb("picked", [P, E])
        den0 = sb("den0", [P, 1])
        den = sb("den", [P, 1])
        rden = sb("rden", [P, 1])
        g = w_raw_all[:, 0:GN]
        gt_hi = w_hi_all[:, 0:2 * GC * P].rearrange("p (a j n) -> p a j n", a=2, j=GC)
        gt_lo = w_lo_all[:, 0:2 * GC * P].rearrange("p (a j n) -> p a j n", a=2, j=GC)

        banks = [bank(f"bank{n}") for n in range(8)]
        ps_p = banks[0:4]
        ps_psmall = banks[4]
        ps_c = banks[5]
        ps_csmall = banks[6][:, 0:SMALL]
        ps_bsmall = banks[3][:, 0:SMALL]
        ps_b = banks[7]
        ps_z = banks[0:2]
        ps_d = banks[2:4]
        ps_s = banks[4]
        ps_ht = banks[5]
        ps_gt = banks[6:8]

        psmall_twice = (ps_psmall[:, 0:KC * SMALL].rearrange("p (m n) -> p m n", m=KC).unsqueeze(1)
                        .to_broadcast([P, 2, KC, SMALL]))

        in_w = [sem(f"in_w{k}") for k in range(KC)]
        in_slots = sem("in_slots")
        in_lora = sem("in_lora")
        in_b = sem("in_b")
        in_xt_first = sem("in_xt_first")
        in_xt_rest = sem("in_xt_rest")
        in_exp = [sem(f"in_exp{q}") for q in range(4)]
        in_xn = sem("in_xn")
        stacked = sem("stacked")
        stored = sem("stored")
        wh_done = sem("wh_done")
        wl_done = sem("wl_done")
        lbh_done = sem("lbh_done")
        lbl_done = sem("lbl_done")
        pe_psmall = sem("pe_psmall")
        phs_done = sem("phs_done")
        pls_done = sem("pls_done")
        pe_p = sem("pe_p")
        ph_done = sem("ph_done")
        pl_done = sem("pl_done")
        pe_c = sem("pe_c")
        ch_done = sem("ch_done")
        cl_done = sem("cl_done")
        bias_step = sem("bias_step")
        bp_done = sem("bp_done")
        pe_bias = sem("pe_bias")
        bias_added = sem("bias_added")
        brh_done = sem("brh_done")
        br_done = sem("br_done")
        eh_done = sem("eh_done")
        el_done = sem("el_done")
        zeroed = sem("zeroed")
        consts = sem("consts")
        first_copied = [sem("first_x_copied"), sem("first_la_copied")]
        then_copied = [sem("then_x_copied"), sem("then_la_copied")]
        x_done = sem("x_done")
        pe_x = sem("pe_x")
        hh_done = sem("hh_done")
        hrep_done = sem("hrep_done")
        hl_done = sem("hl_done")
        pe_ht = sem("pe_ht")
        ht_done = sem("ht_done")
        pe_z = sem("pe_z")
        small_done = sem("small_done")
        max_done = sem("max_done")
        exp_done = sem("exp_done")
        top_done = sem("top_done")
        chosen_done = sem("chosen_done")
        rest_done = sem("rest_done")
        picked_done = sem("picked_done")
        den0_done = sem("den0_done")
        den_done = sem("den_done")
        rden_done = sem("rden_done")
        g_done = sem("g_done")
        acc_done = sem("acc_done")
        pe_gt = sem("pe_gt")
        gh_done = sem("gh_done")
        gl_done = sem("gl_done")
        pe_d = sem("pe_d")
        out_done = sem("out_done")

        block = ctx.enter_context(nc.Block())

        @block.sync
        def _(sp):
            sp.dma_start(slot_row[:, :], slots).then_inc(in_slots, 16)
            for k in range(KC):
                sp.dma_start(w_raw[:, k, :], w_cat[k]).then_inc(in_w[k], 16)
            sp.wait_ge(in_slots, 16)
            for t in range(NT):
                slot = sp.value_load(slot_row[0:1, t:t + 1], min_val=0, max_val=SLOTS - 1)
                src = tables[bass.ds(slot, 1), :, :].rearrange("o p n -> p (o n)")
                sp.dma_start(lora_raw[:, t, :], src).then_inc(in_lora, 16)
            sp.dma_start(b1_col[:, :], b1).then_inc(in_b, 16)
            sp.dma_start(b2_row[:, :], b2).then_inc(in_b, 16)
            sp.dma_start(xt_raw[:, 0:2, :], x_t[:, 0:2, :]).then_inc(in_xt_first, 16)
            for q in range(4):
                js = slice(q * GC // 4, (q + 1) * GC // 4)
                sp.dma_start(exp_raw[:, js, :], experts[:, js, :]).then_inc(in_exp[q], 16)
            sp.dma_start(xt_raw[:, 2:NT, :], x_t[:, 2:NT, :]).then_inc(in_xt_rest, 16)
            sp.dma_start(xn[:, :, :], x_n).then_inc(in_xn, 16)
            sp.wait_ge(zeroed, 1)
            sp.wait_ge(ch_done, 2)
            sp.wait_ge(cl_done, 2)
            for t in range(NT):
                for n, part in enumerate((c_hi, c_lo, c_hi, c_lo)):
                    sp.dma_start(c_stack[n * R:(n + 1) * R, t, :].bitcast(F32),
                                 part[t * R:(t + 1) * R, :].bitcast(F32)).then_inc(stacked, 16)
            sp.wait_ge(br_done, 1)
            for n, part in enumerate((br_hi, br_lo)):
                sp.dma_start(c_stack[BIAS_ROW + n:BIAS_ROW + n + 1, :, :].bitcast(F32),
                             part[0:1, :].bitcast(F32).unsqueeze(1).to_broadcast([1, NT, W2N])).then_inc(stacked, 16)
            with sp.Fori(0, NT) as t:
                sp.wait_ge(out_done, t + 1)
                dst = out[bass.ds(t, 1), :, :].rearrange("o p n -> p (o n)")
                src = xn[:, bass.ds(t, 1), :].rearrange("p o n -> p (o n)")
                sp.dma_start(dst, src).then_inc(stored, 16)
            sp.wait_ge(stored, 16 * NT)

        @block.gpsimd
        def _(pool):
            pool.memset(ident[:, :], 0.0).then_inc(consts, 1)
            pool.wait_ge(consts, 1)
            pool.affine_select(out=ident[:, :], in_=ident[:, :], compare_op=ALU.not_equal, fill=1.0,
                               base=0, pattern=[[-1, P]], channel_multiplier=1).then_inc(consts, 1)
            pool.memset(ones[:, :].bitcast(F32), 1.0).then_inc(consts, 1)
            pool.memset(h_stack[:, BIAS_ROW + 2:P], 0.0).then_inc(consts, 1)
            pool.memset(h_stack[:, BIAS_ROW:BIAS_ROW + 2], 1.0).then_inc(consts, 1)
            pool.memset(probs[:, E:E + 8], -1.0).then_inc(consts, 1)
            pool.memset(chosen[:, 2:8], -1.0).then_inc(consts, 1)
            pool.memset(c_stack[:, :, :].bitcast(F32), 0.0).then_inc(zeroed, 1)

            def split_x(t, par, landed, copied, count):
                xt = xt_raw[:, bass.ds(t, 1), :].rearrange("p o n -> p (o n)")
                la = lora_raw[:, bass.ds(t, 1), 0:KC * R].rearrange("p o (k r) -> p (o k) r", k=KC)
                xh = x_hi[:, par].rearrange("p k n -> p (k n)")
                pool.tensor_copy(xh, xt).then_inc(copied[0], 1)
                pool.tensor_copy(mv_hi[:, par, :, 0:R], la).then_inc(copied[1], 1)
                pool.wait_ge(*landed)
                pool.wait_ge(copied[0], count)
                pool.tensor_tensor(x_lo[:, par].rearrange("p k n -> p (k n)"), xt, xh.bitcast(F32),
                                   ALU.subtract).then_inc(x_done, 1)
                pool.wait_ge(in_lora, 16 * NT)
                pool.wait_ge(copied[1], count)
                pool.tensor_tensor(mv_lo[:, par, :, 0:R], la, mv_hi[:, par, :, 0:R].bitcast(F32),
                                   ALU.subtract).then_inc(x_done, 1)

            pool.wait_ge(in_lora, 16 * NT)
            pool.wait_ge(lbh_done, 1)
            pool.tensor_tensor(lb_lo[:, :, :].rearrange("p k (t r) -> p t k r", t=NT),
                               lora_raw[:, :, KC * R:AL].rearrange("p t (k r) -> p t k r", k=KC),
                               lb_hi[:, :, :].rearrange("p k (t r) -> p t k r", t=NT).bitcast(F32),
                               ALU.subtract).then_inc(lbl_done, 1)
            pool.wait_ge(in_xt_first, 16)
            for t in range(2):
                split_x(t, t, (in_xt_first, 16), first_copied, t + 1)
            for q in range(4):
                js = slice(q * GC // 4, (q + 1) * GC // 4)
                pool.wait_ge(eh_done, q + 1)
                pool.tensor_tensor(e_lo[:, js, :], exp_raw[:, js, :], e_hi[:, js, :].bitcast(F32),
                                   ALU.subtract).then_inc(el_done, 1)
            pool.wait_ge(in_xt_rest, 16)
            with pool.Fori(1, NT // 2) as pair:
                t0 = 2 * pair
                for u in range(2):
                    pool.wait_ge(pe_x, t0 + u - 1)
                    split_x(t0 + u, u, (in_xt_rest, 16), then_copied, t0 + u - 1)

        @block.scalar
        def _(act):
            for k in range(KC):
                act.wait_ge(in_w[k], 16)
                nc.scalar.activation(w_hi[:, k, :], w_raw[:, k, :], ACT.Copy).then_inc(wh_done, 1)
            act.wait_ge(in_lora, 16 * NT)
            nc.scalar.activation(lb_hi[:, :, :].rearrange("p k (t r) -> p t k r", t=NT),
                                 lora_raw[:, :, KC * R:AL].rearrange("p t (k r) -> p t k r", k=KC),
                                 ACT.Copy).then_inc(lbh_done, 1)

            def split_experts(q):
                js = slice(q * GC // 4, (q + 1) * GC // 4)
                act.wait_ge(in_exp[q], 16)
                nc.scalar.activation(e_hi[:, js, :], exp_raw[:, js, :], ACT.Copy).then_inc(eh_done, 1)

            split_experts(0)
            split_experts(1)
            act.wait_ge(pe_psmall, 1)
            nc.scalar.activation(mv_hi[:, :, :, R:MVN], psmall_twice, ACT.Copy).then_inc(phs_done, 1)
            for m in range(KC):
                act.wait_ge(pe_p, m + 1)
                nc.scalar.activation(p_hi[:, m, :], ps_p[m][:, :], ACT.Copy).then_inc(ph_done, 1)
            act.wait_ge(pe_c, 1)
            nc.scalar.activation(c_hi[:, 0:D], ps_c[:, :], ACT.Copy).then_inc(ch_done, 1)
            nc.scalar.activation(c_hi[:, D:W2N], ps_csmall, ACT.Copy).then_inc(ch_done, 1)
            split_experts(2)
            split_experts(3)

            def lora_hi(t):
                act.wait_ge(pe_x, t + 1)
                if not (isinstance(t, int) and t == 0):
                    act.wait_ge(pe_ht, t)
                src = ps_s[:, 0:R].unsqueeze(1).to_broadcast([P, 2, R])
                dst = h_stack[:, 0:2 * R].rearrange("p (a r) -> p a r", a=2).bitcast(F32R)
                nc.scalar.activation(dst, src, ACT.Copy, scale=LORA_SCALE).then_inc(hh_done, 1)

            def lora_t(t, par):
                act.wait_ge(pe_ht, t + 1)
                if not (isinstance(t, int) and t < 2):
                    act.wait_ge(pe_z, t - 1)
                nc.scalar.activation(ht[:, par, :], ps_ht[:, 0:P], ACT.Copy).then_inc(ht_done, 1)

            def small_out(t):
                act.wait_ge(pe_z, t + 1)
                if not (isinstance(t, int) and t == 0):
                    act.wait_ge(g_done, t)
                nc.scalar.activation(small[:, :], ps_s[:, R:MVN], ACT.Copy).then_inc(small_done, 1)

            def exps(t):
                act.wait_ge(small_done, t + 1)
                act.wait_ge(max_done, t + 1)
                if not (isinstance(t, int) and t == 0):
                    act.wait_ge(picked_done, t)
                    act.wait_ge(den0_done, t)
                else:
                    act.wait_ge(consts, 7)
                nc.scalar.activation(probs[:, 0:E], small[:, RH:SMALL], ACT.Exp, bias=neg_max[:, 0:1],
                                     accum_out=prob_sum[:, 0:1]).then_inc(exp_done, 1)

            def g_hi(t, par):
                for half in range(2):
                    act.wait_ge(pe_gt, 2 * t + half + 1)
                    dst = gt_hi[:, par, half * GC // 2:(half + 1) * GC // 2, :]
                    nc.scalar.activation(dst.rearrange("p j n -> p (j n)"), ps_gt[half][:, :],
                                         ACT.Copy).then_inc(gh_done, 1)

            for t in range(2):
                lora_hi(t)
                lora_t(t, t)
                small_out(t)
                exps(t)
            g_hi(0, 0)
            with act.Fori(0, NT // 2 - 1) as pair:
                t0 = 2 * pair
                for u in range(2):
                    t = t0 + u
                    lora_hi(t + 2)
                    lora_t(t + 2, u)
                    g_hi(t + 1, 1 - u)
                    small_out(t + 2)
                    exps(t + 2)
            g_hi(NT - 1, (NT - 1) % 2)

        @block.vector
        def _(dve):
            for k in range(KC):
                dve.wait_ge(wh_done, k + 1)
                nc.vector.tensor_tensor(w_lo[:, k, :], w_raw[:, k, :], w_hi[:, k, :].bitcast(F32),
                                        ALU.subtract).then_inc(wl_done, 1)
            dve.wait_ge(in_b, 32)
            nc.vector.tensor_scalar(bias_part[:, :], w_raw[:, 0, D:], b1_col[:, 0:1], None,
                                    ALU.mult).then_inc(bias_step, 1)
            for k in range(1, KC):
                dve.wait_ge(bias_step, k)
                nc.vector.scalar_tensor_tensor(out=bias_part[:, :], in0=w_raw[:, k, D:],
                                               scalar=b1_col[:, k:k + 1], in1=bias_part[:, :],
                                               op0=ALU.mult, op1=ALU.add).then_inc(bias_step, 1)
            dve.wait_ge(bias_step, KC)
            nc.vector.tensor_copy(bp_hi[:, :], bias_part[:, :]).then_inc(bp_done, 1)
            dve.wait_ge(bp_done, 1)
            nc.vector.tensor_tensor(bp_lo[:, :], bias_part[:, :], bp_hi[:, :].bitcast(F32),
                                    ALU.subtract).then_inc(bp_done, 1)
            dve.wait_ge(phs_done, 1)
            nc.vector.tensor_tensor(mv_lo[:, :, :, R:MVN], psmall_twice,
                                    mv_hi[:, :, :, R:MVN].bitcast(F32), ALU.subtract).then_inc(pls_done, 1)
            for m in range(KC):
                dve.wait_ge(ph_done, m + 1)
                nc.vector.tensor_tensor(p_lo[:, m, :], ps_p[m][:, :], p_hi[:, m, :].bitcast(F32),
                                        ALU.subtract).then_inc(pl_done, 1)
            dve.wait_ge(ch_done, 1)
            nc.vector.tensor_tensor(c_lo[:, 0:D], ps_c[:, :], c_hi[:, 0:D].bitcast(F32),
                                    ALU.subtract).then_inc(cl_done, 1)
            dve.wait_ge(ch_done, 2)
            nc.vector.tensor_tensor(c_lo[:, D:W2N], ps_csmall, c_hi[:, D:W2N].bitcast(F32),
                                    ALU.subtract).then_inc(cl_done, 1)
            dve.wait_ge(pe_bias, 1)
            nc.vector.tensor_tensor(bias_row[0:1, 0:D], ps_b[0:1, :], b2_row[0:1, :],
                                    ALU.add).then_inc(bias_added, 1)
            nc.vector.tensor_copy(bias_row[0:1, D:W2N], ps_bsmall[0:1, :]).then_inc(bias_added, 1)
            dve.wait_ge(bias_added, 2)
            nc.vector.tensor_copy(br_hi[0:1, :], bias_row[0:1, :]).then_inc(brh_done, 1)
            dve.wait_ge(brh_done, 1)
            nc.vector.tensor_tensor(br_lo[0:1, :], bias_row[0:1, :], br_hi[0:1, :].bitcast(F32),
                                    ALU.subtract).then_inc(br_done, 1)

            def lora_lo(t):
                dve.wait_ge(hh_done, t + 1)
                nc.vector.scalar_tensor_tensor(
                    out=h_stack[:, 2 * R:4 * R].rearrange("p (a r) -> p a r", a=2).bitcast(F32R),
                    in0=ps_s[:, 0:R].unsqueeze(1).to_broadcast([P, 2, R]), scalar=LORA_SCALE,
                    in1=h_stack[:, 0:2 * R].rearrange("p (a r) -> p a r", a=2),
                    op0=ALU.mult, op1=ALU.subtract).then_inc(hl_done, 1)

            def route(t):
                xt = xn[:, bass.ds(t, 1), :].rearrange("p o n -> p (o n)")
                dve.wait_ge(small_done, t + 1)
                if not (isinstance(t, int) and t == 0):
                    dve.wait_ge(exp_done, t)
                nc.vector.tensor_reduce(neg_max[:, :], small[:, RH:SMALL], AX_X, ALU.max,
                                        negate=True).then_inc(max_done, 1)
                nc.vector.tensor_tensor(xt, ps_z_of(t), xt, ALU.add).then_inc(acc_done, 1)
                dve.wait_ge(consts, 7)
                dve.wait_ge(exp_done, t + 1)
                nc.vector.max(top8[:, :], probs[:, :]).then_inc(top_done, 1)
                dve.wait_ge(top_done, t + 1)
                nc.vector.tensor_copy(chosen[:, 0:2], top8[:, 0:2]).then_inc(chosen_done, 1)
                nc.vector.tensor_scalar(den0[:, :], prob_sum[:, :], TOPW_EPS, top8[:, 0:1],
                                        ALU.mult, ALU.add).then_inc(den0_done, 1)
                dve.wait_ge(consts, 7)
                dve.wait_ge(chosen_done, t + 1)
                nc.vector.match_replace(rest[:, :], chosen[:, :], probs[:, :], 0.0).then_inc(rest_done, 1)
                dve.wait_ge(den0_done, t + 1)
                nc.vector.tensor_scalar(den[:, :], den0[:, :], top8[:, 1:2], 1.0 / DELTA_SCALE,
                                        ALU.add, ALU.mult).then_inc(den_done, 1)
                dve.wait_ge(rest_done, t + 1)
                nc.vector.tensor_tensor(picked[:, :], probs[:, 0:E], rest[:, 0:E],
                                        ALU.subtract).then_inc(picked_done, 1)
                dve.wait_ge(den_done, t + 1)
                nc.vector.reciprocal(rden[:, :], den[:, :]).then_inc(rden_done, 1)
                dve.wait_ge(picked_done, t + 1)
                dve.wait_ge(rden_done, t + 1)
                if not (isinstance(t, int) and t == 0):
                    dve.wait_ge(pe_gt, 2 * t)
                nc.vector.scalar_tensor_tensor(
                    out=g[:, :].rearrange("p (e r) -> p e r", e=E),
                    in0=small[:, 0:RH].unsqueeze(1).to_broadcast([P, E, RH]), scalar=rden[:, 0:1],
                    in1=picked[:, :].unsqueeze(2).to_broadcast([P, E, RH]),
                    op0=ALU.mult, op1=ALU.mult).then_inc(g_done, 1)

            parity = [0]

            def ps_z_of(t):
                return ps_z[parity[0]][:, :]

            def g_lo(t, par):
                for half in range(2):
                    dve.wait_ge(gh_done, 2 * t + half + 1)
                    js = slice(half * GC // 2, (half + 1) * GC // 2)
                    nc.vector.tensor_tensor(gt_lo[:, par, js, :].rearrange("p j n -> p (j n)"),
                                            ps_gt[half][:, :],
                                            gt_hi[:, par, js, :].rearrange("p j n -> p (j n)").bitcast(F32),
                                            ALU.subtract).then_inc(gl_done, 1)

            def finish(t, par):
                dve.wait_ge(pe_d, t + 1)
                dve.wait_ge(acc_done, t + 1)
                xt = xn[:, bass.ds(t, 1), :].rearrange("p o n -> p (o n)")
                nc.vector.tensor_tensor(xt, ps_d[par][:, :], xt, ALU.add).then_inc(out_done, 1)

            dve.wait_ge(in_xn, 16)
            dve.wait_ge(consts, 7)
            for t in range(2):
                lora_lo(t)
                parity[0] = t
                route(t)
            g_lo(0, 0)
            with dve.Fori(0, NT // 2 - 1) as pair:
                t0 = 2 * pair
                for u in range(2):
                    t = t0 + u
                    lora_lo(t + 2)
                    g_lo(t + 1, 1 - u)
                    parity[0] = u
                    route(t + 2)
                    finish(t, u)
            g_lo(NT - 1, (NT - 1) % 2)
            for t in range(NT - 2, NT):
                finish(t, t % 2)

        @block.tensor
        def _(pe):
            def three(out_ap, hi, lo, mv_h, mv_l, first, last):
                mm(out_ap, hi, mv_h, first, False)
                mm(out_ap, hi, mv_l, False, False)
                return mm(out_ap, lo, mv_h, False, last)

            def mm(out_ap, lhs, rhs, first, last):
                return nc.tensor.matmul(out_ap, lhs, rhs, start=first, stop=last, skip_group_check=True)

            for k in range(KC):
                pe.wait_ge(wh_done, k + 1)
                pe.wait_ge(wl_done, k + 1)
                for m in range(KC):
                    cols = slice(m * P, (m + 1) * P)
                    last = three(ps_psmall[:, m * SMALL:(m + 1) * SMALL], w_hi[:, k, cols], w_lo[:, k, cols],
                                 w_hi[:, k, 2 * D:], w_lo[:, k, 2 * D:], k == 0 and m == 0, k == KC - 1)
                if k == KC - 1:
                    last.then_inc(pe_psmall, 1)
                for m in range(KC):
                    cols = slice(m * P, (m + 1) * P)
                    last = three(ps_p[m][:, :], w_hi[:, k, cols], w_lo[:, k, cols], w_hi[:, k, D:2 * D],
                                 w_lo[:, k, D:2 * D], k == 0, k == KC - 1)
                    if k == KC - 1:
                        last.then_inc(pe_p, 1)
            pe.wait_ge(lbh_done, 1)
            pe.wait_ge(lbl_done, 1)
            for k in range(KC):
                three(ps_c[:, :], lb_hi[:, k, :], lb_lo[:, k, :], w_hi[:, k, D:2 * D],
                      w_lo[:, k, D:2 * D], k == 0, k == KC - 1)
                last = three(ps_csmall, lb_hi[:, k, :], lb_lo[:, k, :], w_hi[:, k, 2 * D:],
                             w_lo[:, k, 2 * D:], k == 0, k == KC - 1)
            last.then_inc(pe_c, 1)
            pe.wait_ge(consts, 7)
            pe.wait_ge(bp_done, 2)
            pe.wait_ge(pl_done, KC)
            mm(ps_b[:, :], ones[:, :], bp_hi[:, 0:D], True, False)
            mm(ps_b[:, :], ones[:, :], bp_lo[:, 0:D], False, True)
            mm(ps_bsmall, ones[:, :], bp_hi[:, D:], True, False)
            mm(ps_bsmall, ones[:, :], bp_lo[:, D:], False, True).then_inc(pe_bias, 1)

            def x_products(t, par):
                pe.wait_ge(x_done, 2 * t + 2)
                first_tile = isinstance(t, int) and t == 0
                if not (isinstance(t, int) and t < 2):
                    pe.wait_ge(acc_done, t - 1)
                if not first_tile:
                    pe.wait_ge(small_done, t)
                else:
                    pe.wait_ge(pls_done, 1)
                for k in range(KC):
                    hi, lo = x_hi[:, par, k, :], x_lo[:, par, k, :]
                    three(ps_z[par][:, :], hi, lo, p_hi[:, k, :], p_lo[:, k, :], k == 0, k == KC - 1)
                    last = three(ps_s[:, 0:MVN], hi, lo, mv_hi[:, par, k, :], mv_lo[:, par, k, :],
                                 k == 0, k == KC - 1)
                last.then_inc(pe_x, 1)

            def lora_transpose(t):
                pe.wait_ge(hh_done, t + 1)
                pe.wait_ge(hl_done, t + 1)
                if isinstance(t, int) and t == 0:
                    pe.wait_ge(cl_done, 2)
                else:
                    pe.wait_ge(ht_done, t)
                nc.tensor.transpose(ps_ht[:, 0:P], h_stack[:, :], ident[:, :]).then_inc(pe_ht, 1)

            def lora_product(t, par):
                pe.wait_ge(ht_done, t + 1)
                if isinstance(t, int) and t == 0:
                    pe.wait_ge(stacked, 16 * (4 * NT + 2))
                rows = c_stack[:, bass.ds(t, 1), :].rearrange("p o n -> p (o n)")
                mm(ps_z[par][:, :], ht[:, par, :], rows[:, 0:D], False, True)
                mm(ps_s[:, R:MVN], ht[:, par, :], rows[:, D:W2N], False, True).then_inc(pe_z, 1)

            def g_transpose(t):
                pe.wait_ge(g_done, t + 1)
                first_tile = isinstance(t, int) and t == 0
                for half in range(2):
                    if first_tile:
                        pe.wait_ge(br_done, 1)
                    else:
                        pe.wait_ge(gl_done, 2 * t + half - 1)
                    for j in range(GC // 2):
                        c = half * GC // 2 + j
                        last = nc.tensor.transpose(ps_gt[half][:, j * P:(j + 1) * P],
                                                   g[:, c * P:(c + 1) * P], ident[:, :])
                    last.then_inc(pe_gt, 1)

            def experts_product(t, par, chunks):
                if chunks[0] == 0:
                    pe.wait_ge(gh_done, 2 * t + 2)
                    pe.wait_ge(gl_done, 2 * t + 2)
                for c in chunks:
                    last = three(ps_d[par][:, :], gt_hi[:, par, c, :], gt_lo[:, par, c, :],
                                 e_hi[:, c, :], e_lo[:, c, :], c == 0, c == GC - 1)
                if chunks[-1] == GC - 1:
                    last.then_inc(pe_d, 1)

            for t in range(2):
                x_products(t, t)
                lora_transpose(t)
                lora_product(t, t)
            g_transpose(0)
            pe.wait_ge(eh_done, 4)
            pe.wait_ge(el_done, 4)

            def iteration(t, par, more, after):
                if more:
                    x_products(t + 2, par)
                experts_product(t, par, (0, 1, 2))
                if more:
                    lora_transpose(t + 2)
                if after:
                    g_transpose(t + 1)
                experts_product(t, par, (3, 4, 5))
                if more:
                    lora_product(t + 2, par)
                experts_product(t, par, (6, 7))

            with pe.Fori(0, NT // 2 - 1) as pair:
                t0 = 2 * pair
                for u in range(2):
                    iteration(t0 + u, u, True, True)
            iteration(NT - 2, 0, False, True)
            iteration(NT - 1, 1, False, False)


def kernel(x, itok_B_0_23, L0_cond_W, L0_cond_b, L0_cond_lora_As, L0_cond_lora_Bs, L0_ffn_base_w,
           L0_ffn_base_b, L0_ffn_A, L0_ffn_B, L0_ffn_router_w):
    import numpy as np
    import concourse.bacc as bacc
    from concourse.bass_utils import run_bass_kernel_spmd

    c = np.ascontiguousarray
    x = np.asarray(x)
    x_t = c(x.reshape(NT, P, KC, P).transpose(3, 0, 2, 1).reshape(P, NT, KC * P))
    x_n = c(x.transpose(1, 0, 2))
    w2 = np.concatenate([np.asarray(L0_ffn_base_w).T, np.asarray(L0_ffn_A).T,
                         np.asarray(L0_ffn_router_w).T], axis=1)
    w_cat = c(np.concatenate([np.asarray(L0_cond_W), w2], axis=1).reshape(KC, P, D + W2N))
    a = np.asarray(L0_cond_lora_As).reshape(SLOTS, KC, P, R).transpose(0, 2, 1, 3).reshape(SLOTS, P, KC * R)
    b = np.asarray(L0_cond_lora_Bs).reshape(SLOTS, R, KC, P).transpose(0, 3, 2, 1).reshape(SLOTS, P, KC * R)
    tables = c(np.concatenate([a, b], axis=2))
    ex = np.asarray(L0_ffn_B).transpose(0, 2, 1).reshape(GC, P, D)
    arrays = {
        "x_t": x_t, "x_n": x_n, "w_cat": w_cat, "tables": tables,
        "slots": c(np.asarray(itok_B_0_23).reshape(1, NT)),
        "b1": c(np.asarray(L0_cond_b).reshape(KC, P).T), "b2": c(np.asarray(L0_ffn_base_b).reshape(1, D)),
        "experts": c(ex.transpose(1, 0, 2)),
    }
    nc = bacc.Bacc("TRN2", target_bir_lowering=False, num_devices=1)
    aps = [nc.dram_tensor(n, v.shape, mybir.dt.from_np(v.dtype), kind="ExternalInput").ap()
           for n, v in arrays.items()]
    out = nc.dram_tensor("out", (NT, P, D), F32, kind="ExternalOutput").ap()
    adaln_ffn_kernel(nc, *aps, out)
    r = run_bass_kernel_spmd(nc, [arrays], core_ids=[0])
    return r.results[0]["out"]
```

```python
from contextlib import ExitStack

import concourse.bass as bass
from concourse import mybir

F32 = mybir.dt.float32
F32R = mybir.dt.float32r
I32 = mybir.dt.int32
ALU = mybir.AluOpType
ACT = mybir.ActivationFunctionType
AX_X = mybir.AxisListType.X

P = 128
NT = 8
D = 512
KC = D // P
R = 16
RH = 64
E = 16
SMALL = RH + E
W2N = D + SMALL
MVN = R + W2N
W2H = W2N // 2
MVH = MVN // 2
BANK = 512
GN = E * RH
GC = GN // P
SLOTS = 32
AL = 2 * KC * R
LORA_SCALE = 2.0
DELTA_SCALE = 0.5
TOPW_EPS = 1e-6
BIAS_ROW = 3 * R
WARM_UP = 11


def adaln_ffn_kernel(nc, x_t, x_n, w_cat, tables, slots, b1, b2, experts, out):
    with ExitStack() as ctx:
        def sb(name, shape, dt=F32):
            return ctx.enter_context(nc.sbuf_tensor(name, shape, dt))

        def bank(name, shape=(P, D)):
            return ctx.enter_context(nc.psum_tensor(name, list(shape), F32))

        def sem(name):
            return ctx.enter_context(nc.semaphore(name))

        xt_raw = sb("xt_raw", [P, NT, KC * P])
        xn = sb("xn", [P, NT, D])
        w_raw_all = sb("w_raw_all", [P, KC * (D + W2N)])
        w_raw = w_raw_all[:, :].rearrange("p (k n) -> p k n", k=KC)
        lora_raw = sb("lora_raw", [P, NT, AL])
        exp_raw = sb("exp_raw", [P, GC, D])
        slot_row = sb("slot_row", [1, NT], I32)
        b1_col = sb("b1_col", [P, KC])
        b2_row = sb("b2_row", [1, D])
        w_hi_all = sb("w_hi_all", [P, KC * (D + W2N)], F32R)
        w_lo_all = sb("w_lo_all", [P, KC * (D + W2N)], F32R)
        w_hi = w_hi_all[:, :].rearrange("p (k n) -> p k n", k=KC)
        w_lo = w_lo_all[:, :].rearrange("p (k n) -> p k n", k=KC)
        lb_hi = sb("lb_hi", [P, KC, NT * R], F32R)
        lb_lo = sb("lb_lo", [P, KC, NT * R], F32R)
        p_hi = sb("p_hi", [P, KC, MVN], F32R)
        p_lo = sb("p_lo", [P, KC, MVN], F32R)
        c_hi = sb("c_hi", [P, W2N], F32R)
        c_lo = sb("c_lo", [P, W2N], F32R)
        bias_part = sb("bias_part", [P, W2N])
        bp_hi = sb("bp_hi", [P, W2N], F32R)
        bp_lo = sb("bp_lo", [P, W2N], F32R)
        br_hi = bp_hi[0:1, :]
        br_lo = bp_lo[0:1, :]
        c_stack = sb("c_stack", [P, NT, W2N], F32R)
        e_hi = sb("e_hi", [P, GC, D], F32R)
        e_lo = sb("e_lo", [P, GC, D], F32R)
        x_hi = sb("x_hi", [P, 2, KC, P], F32R)
        x_lo = sb("x_lo", [P, 2, KC, P], F32R)
        ident = sb("ident", [P, P])
        ones = sb("ones", [P, P], F32R)
        zeros = e_hi[:, 0, :]
        h_stack = sb("h_stack", [P, P])
        ht = sb("ht", [P, 2, P], F32R)
        small = sb("small", [P, SMALL])
        neg_max = sb("neg_max", [P, 1])
        probs = sb("probs", [P, E + 8])
        prob_sum = sb("prob_sum", [P, 1])
        top8 = sb("top8", [P, 8])
        chosen = sb("chosen", [P, 8])
        rest = sb("rest", [P, E + 8])
        picked = sb("picked", [P, E])
        den0 = sb("den0", [P, 1])
        den = sb("den", [P, 1])
        rden = sb("rden", [P, 1])
        g = w_raw_all[:, 0:GN]
        gt_hi = w_hi_all[:, 0:2 * GC * P].rearrange("p (a j n) -> p a j n", a=2, j=GC)
        gt_lo = w_lo_all[:, 0:2 * GC * P].rearrange("p (a j n) -> p a j n", a=2, j=GC)

        pairs = [bank(f"pair{n}", (P, 2 * BANK)) for n in range(4)]
        ps_c = pairs[0]
        ps_b = pairs[1]
        ps_z = pairs[0:2]
        ps_d = [pairs[2][:, 0:BANK], pairs[2][:, BANK:]]
        ps_gt = [pairs[3][:, 0:BANK], pairs[3][:, BANK:]]
        ps_ht = ps_gt[0][:, 0:P]

        def w2_cols(ps):
            return ps[:, BANK - W2H:BANK + W2H]

        z_lora = BANK - MVH
        z_small = z_lora + R
        z_base = z_small + SMALL

        in_w = [sem(f"in_w{k}") for k in range(KC)]
        in_slots = sem("in_slots")
        in_lora = sem("in_lora")
        in_b = sem("in_b")
        in_xt_first = sem("in_xt_first")
        in_xt_rest = sem("in_xt_rest")
        in_exp = [sem(f"in_exp{q}") for q in range(4)]
        in_xn = sem("in_xn")
        stacked = [sem("stacked_even"), sem("stacked_odd")]
        stacked_bias = sem("stacked_bias")
        stored = sem("stored")
        wh_first = sem("wh_first")
        wh_done = sem("wh_done")
        wl_done = sem("wl_done")
        lbh_done = sem("lbh_done")
        lbl_done = sem("lbl_done")
        pe_p = sem("pe_p")
        ph_done = sem("ph_done")
        pl_done = sem("pl_done")
        pe_c = sem("pe_c")
        ch_done = sem("ch_done")
        cl_done = sem("cl_done")
        bias_step = sem("bias_step")
        bp_done = sem("bp_done")
        pe_bias = sem("pe_bias")
        brh_done = sem("brh_done")
        br_done = sem("br_done")
        eh_done = sem("eh_done")
        el_gpsimd = sem("el_gpsimd")
        el_vector = sem("el_vector")
        warm = sem("warm")
        pe_warm = sem("pe_warm")
        zeroed = sem("zeroed")
        consts = sem("consts")
        first_copied = [sem("first_x_copied"), sem("first_la_copied")]
        then_copied = [sem("then_x_copied"), sem("then_la_copied")]
        x_done = sem("x_done")
        pe_left = sem("pe_left")
        pe_x = sem("pe_x")
        hh_done = sem("hh_done")
        hrep_done = sem("hrep_done")
        hl_done = sem("hl_done")
        pe_ht = sem("pe_ht")
        ht_done = sem("ht_done")
        pe_z = sem("pe_z")
        small_done = sem("small_done")
        max_done = sem("max_done")
        exp_done = sem("exp_done")
        top_done = sem("top_done")
        chosen_done = sem("chosen_done")
        rest_done = sem("rest_done")
        picked_done = sem("picked_done")
        den0_done = sem("den0_done")
        den_done = sem("den_done")
        rden_done = sem("rden_done")
        g_done = sem("g_done")
        acc_done = sem("acc_done")
        pe_gt = sem("pe_gt")
        gh_done = sem("gh_done")
        gl_done = sem("gl_done")
        pe_d = sem("pe_d")
        out_done = sem("out_done")

        block = ctx.enter_context(nc.Block())

        @block.sync
        def _(sp):
            sp.dma_start(slot_row[:, :], slots).then_inc(in_slots, 16)
            for k in range(KC):
                sp.dma_start(w_raw[:, k, :], w_cat[k]).then_inc(in_w[k], 16)
            sp.dma_start(b1_col[:, :], b1).then_inc(in_b, 16)
            sp.dma_start(b2_row[:, :], b2).then_inc(in_b, 16)
            sp.dma_start(xt_raw[:, 0:2, :], x_t[:, 0:2, :]).then_inc(in_xt_first, 16)

            def load_experts(q):
                js = slice(q * GC // 4, (q + 1) * GC // 4)
                sp.dma_start(exp_raw[:, js, :], experts[:, js, :]).then_inc(in_exp[q], 16)

            load_experts(0)
            load_experts(1)
            sp.wait_ge(in_slots, 16)
            for t in range(NT):
                slot = sp.value_load(slot_row[0:1, t:t + 1], min_val=0, max_val=SLOTS - 1)
                src = tables[bass.ds(slot, 1), :, :].rearrange("o p n -> p (o n)")
                sp.dma_start(lora_raw[:, t, :], src).then_inc(in_lora, 16)
            load_experts(2)
            load_experts(3)
            sp.dma_start(xn[:, :, :], x_n).then_inc(in_xn, 16)
            sp.dma_start(xt_raw[:, 2:NT, :], x_t[:, 2:NT, :]).then_inc(in_xt_rest, 16)

            def stack(t):
                if t >= 2:
                    sp.wait_ge(stacked[t % 2], 48 * (t // 2))
                for n, part in enumerate((c_hi, c_lo, c_hi)):
                    sp.dma_start(c_stack[n * R:(n + 1) * R, t, :].bitcast(F32),
                                 part[t * R:(t + 1) * R, :].bitcast(F32)).then_inc(stacked[t % 2], 16)

            sp.wait_ge(zeroed, 1)
            sp.wait_ge(ch_done, 1)
            sp.wait_ge(cl_done, 1)
            stack(0)
            sp.wait_ge(brh_done, 1)
            sp.wait_ge(br_done, 1)
            for n, part in enumerate((br_hi, br_lo)):
                sp.dma_start(c_stack[BIAS_ROW + n:BIAS_ROW + n + 1, :, :].bitcast(F32),
                             part[0:1, :].bitcast(F32).unsqueeze(1)
                             .to_broadcast([1, NT, W2N])).then_inc(stacked_bias, 16)
            for t in range(1, NT):
                stack(t)
            with sp.Fori(0, NT) as t:
                sp.wait_ge(out_done, t + 1)
                dst = out[bass.ds(t, 1), :, :].rearrange("o p n -> p (o n)")
                src = xn[:, bass.ds(t, 1), :].rearrange("p o n -> p (o n)")
                sp.dma_start(dst, src).then_inc(stored, 16)
            sp.wait_ge(stored, 16 * NT)

        @block.gpsimd
        def _(pool):
            pool.memset(ident[:, :], 0.0).then_inc(consts, 1)
            pool.wait_ge(consts, 1)
            pool.affine_select(out=ident[:, :], in_=ident[:, :], compare_op=ALU.not_equal, fill=1.0,
                               base=0, pattern=[[-1, P]], channel_multiplier=1).then_inc(consts, 1)
            pool.memset(ones[:, :].bitcast(F32), 1.0).then_inc(consts, 1)
            pool.memset(h_stack[:, BIAS_ROW + 2:P], 0.0).then_inc(consts, 1)
            pool.memset(h_stack[:, BIAS_ROW:BIAS_ROW + 2], 1.0).then_inc(consts, 1)
            pool.memset(probs[:, E:E + 8], -1.0).then_inc(consts, 1)
            pool.memset(chosen[:, 2:8], -1.0).then_inc(consts, 1)
            pool.memset(c_stack[:, :, :].bitcast(F32), 0.0).then_inc(zeroed, 1)

            def split_x(t, par, landed, copied, count):
                xt = xt_raw[:, bass.ds(t, 1), :].rearrange("p o n -> p (o n)")
                la = lora_raw[:, bass.ds(t, 1), 0:KC * R].rearrange("p o (k r) -> p (o k) r", k=KC)
                xh = x_hi[:, par].rearrange("p k n -> p (k n)")
                pool.tensor_copy(xh, xt).then_inc(copied[0], 1)
                pool.wait_ge(*landed)
                pool.wait_ge(copied[0], count)
                pool.tensor_tensor(x_lo[:, par].rearrange("p k n -> p (k n)"), xt, xh.bitcast(F32),
                                   ALU.subtract).then_inc(x_done, 1)
                if not (isinstance(t, int) and t == 0):
                    pool.wait_ge(pe_left, t)
                pool.tensor_copy(p_hi[:, :, 0:R], la).then_inc(copied[1], 1)
                pool.wait_ge(in_lora, 16 * NT)
                pool.wait_ge(copied[1], count)
                pool.tensor_tensor(p_lo[:, :, 0:R], la, p_hi[:, :, 0:R].bitcast(F32),
                                   ALU.subtract).then_inc(x_done, 1)

            pool.wait_ge(in_lora, 16 * NT)
            pool.wait_ge(lbh_done, 1)
            pool.tensor_tensor(lb_lo[:, :, :].rearrange("p k (t r) -> p t k r", t=NT),
                               lora_raw[:, :, KC * R:AL].rearrange("p t (k r) -> p t k r", k=KC),
                               lb_hi[:, :, :].rearrange("p k (t r) -> p t k r", t=NT).bitcast(F32),
                               ALU.subtract).then_inc(lbl_done, 1)
            pool.wait_ge(in_xt_first, 16)
            split_x(0, 0, (in_xt_first, 16), first_copied, 1)

            def split_experts_lo(q):
                js = slice(q * GC // 4, (q + 1) * GC // 4)
                pool.wait_ge(eh_done, q + 1)
                pool.tensor_tensor(e_lo[:, js, :], exp_raw[:, js, :], e_hi[:, js, :].bitcast(F32),
                                   ALU.subtract).then_inc(el_gpsimd, 1)

            split_x(1, 1, (in_xt_first, 16), first_copied, 2)
            split_experts_lo(0)
            split_experts_lo(1)
            pool.wait_ge(in_xt_rest, 16)
            with pool.Fori(1, NT // 2) as pair:
                t0 = 2 * pair
                for u in range(2):
                    pool.wait_ge(pe_x, t0 + u - 1)
                    split_x(t0 + u, u, (in_xt_rest, 16), then_copied, t0 + u - 1)

        @block.scalar
        def _(act):
            act.wait_ge(in_w[0], 16)
            nc.scalar.activation(w_hi[:, 0, 0:D], w_raw[:, 0, 0:D], ACT.Copy).then_inc(wh_done, 1)
            for k in range(1, KC):
                act.wait_ge(in_w[k], 16)
                nc.scalar.activation(w_hi[:, k, :], w_raw[:, k, :], ACT.Copy).then_inc(wh_done, 1)
            def split_experts(q):
                js = slice(q * GC // 4, (q + 1) * GC // 4)
                act.wait_ge(in_exp[q], 16)
                nc.scalar.activation(e_hi[:, js, :], exp_raw[:, js, :], ACT.Copy).then_inc(eh_done, 1)

            def folded_hi(m):
                act.wait_ge(pe_p, m + 1)
                nc.scalar.activation(p_hi[:, m, R:], w2_cols(pairs[m]), ACT.Copy).then_inc(ph_done, 1)

            act.wait_ge(pe_warm, 1)
            split_experts(0)
            act.wait_ge(in_lora, 16 * NT)
            nc.scalar.activation(lb_hi[:, :, :].rearrange("p k (t r) -> p t k r", t=NT),
                                 lora_raw[:, :, KC * R:AL].rearrange("p t (k r) -> p t k r", k=KC),
                                 ACT.Copy).then_inc(lbh_done, 1)
            split_experts(1)
            folded_hi(0)
            folded_hi(1)
            folded_hi(2)
            act.wait_ge(pe_c, 1)
            nc.scalar.activation(c_hi[:, :], w2_cols(ps_c), ACT.Copy).then_inc(ch_done, 1)
            act.wait_ge(pe_bias, 1)
            nc.scalar.activation(br_hi, w2_cols(ps_b)[0:1, :], ACT.Copy).then_inc(brh_done, 1)
            folded_hi(3)
            split_experts(2)
            split_experts(3)

            def lora_hi(t, par):
                act.wait_ge(pe_left, t + 1)
                if not (isinstance(t, int) and t == 0):
                    act.wait_ge(pe_ht, t)
                src = ps_z[par][:, z_lora:z_small].unsqueeze(1).to_broadcast([P, 2, R])
                dst = h_stack[:, 0:2 * R].rearrange("p (a r) -> p a r", a=2).bitcast(F32R)
                nc.scalar.activation(dst, src, ACT.Copy, scale=LORA_SCALE).then_inc(hh_done, 1)

            def lora_t(t, par):
                act.wait_ge(pe_ht, t + 1)
                if not (isinstance(t, int) and t < 2):
                    act.wait_ge(pe_z, t - 1)
                nc.scalar.activation(ht[:, par, :], ps_ht, ACT.Copy).then_inc(ht_done, 1)

            def small_out(t, par):
                act.wait_ge(pe_z, t + 1)
                if not (isinstance(t, int) and t == 0):
                    act.wait_ge(g_done, 2 * t)
                nc.scalar.activation(small[:, :], ps_z[par][:, z_small:z_base], ACT.Copy).then_inc(small_done, 1)

            def exps(t):
                act.wait_ge(small_done, t + 1)
                act.wait_ge(max_done, t + 1)
                if not (isinstance(t, int) and t == 0):
                    act.wait_ge(picked_done, t)
                    act.wait_ge(den0_done, t)
                else:
                    act.wait_ge(consts, 7)
                nc.scalar.activation(probs[:, 0:E], small[:, RH:SMALL], ACT.Exp, bias=neg_max[:, 0:1],
                                     accum_out=prob_sum[:, 0:1]).then_inc(exp_done, 1)

            def g_hi(t, par):
                for half in range(2):
                    act.wait_ge(pe_gt, 2 * t + half + 1)
                    dst = gt_hi[:, par, half * GC // 2:(half + 1) * GC // 2, :]
                    nc.scalar.activation(dst.rearrange("p j n -> p (j n)"), ps_gt[half],
                                         ACT.Copy).then_inc(gh_done, 1)

            for t in range(2):
                lora_hi(t, t)
                lora_t(t, t)
                small_out(t, t)
                exps(t)
            g_hi(0, 0)
            with act.Fori(0, NT // 2 - 1) as pair:
                t0 = 2 * pair
                for u in range(2):
                    t = t0 + u
                    lora_hi(t + 2, u)
                    lora_t(t + 2, u)
                    g_hi(t + 1, 1 - u)
                    small_out(t + 2, u)
                    exps(t + 2)
            g_hi(NT - 1, (NT - 1) % 2)

        @block.vector
        def _(dve):
            nc.vector.memset(zeros.bitcast(F32), 0.0).then_inc(warm, 1)
            dve.wait_ge(in_w[0], 16)
            nc.vector.tensor_copy(w_hi[:, 0, D:], w_raw[:, 0, D:]).then_inc(wh_first, 1)
            dve.wait_ge(wh_first, 1)
            for k in range(KC):
                dve.wait_ge(wh_done, k + 1)
                nc.vector.tensor_tensor(w_lo[:, k, :], w_raw[:, k, :], w_hi[:, k, :].bitcast(F32),
                                        ALU.subtract).then_inc(wl_done, 1)
            dve.wait_ge(in_b, 32)
            nc.vector.tensor_scalar(bias_part[:, :], w_raw[:, 0, D:], b1_col[:, 0:1], None,
                                    ALU.mult).then_inc(bias_step, 1)
            for k in range(1, KC):
                dve.wait_ge(bias_step, k)
                nc.vector.scalar_tensor_tensor(out=bias_part[:, :], in0=w_raw[:, k, D:],
                                               scalar=b1_col[:, k:k + 1], in1=bias_part[:, :],
                                               op0=ALU.mult, op1=ALU.add).then_inc(bias_step, 1)
            dve.wait_ge(bias_step, KC)
            nc.vector.tensor_tensor(bias_part[0:1, SMALL:], bias_part[0:1, SMALL:], b2_row[0:1, :],
                                    ALU.add).then_inc(bias_step, 1)
            dve.wait_ge(bias_step, KC + 1)
            nc.vector.tensor_copy(bp_hi[:, :], bias_part[:, :]).then_inc(bp_done, 1)
            dve.wait_ge(bp_done, 1)
            nc.vector.tensor_tensor(bp_lo[:, :], bias_part[:, :], bp_hi[:, :].bitcast(F32),
                                    ALU.subtract).then_inc(bp_done, 1)

            def folded_lo(m):
                dve.wait_ge(ph_done, m + 1)
                nc.vector.tensor_tensor(p_lo[:, m, R:], w2_cols(pairs[m]), p_hi[:, m, R:].bitcast(F32),
                                        ALU.subtract).then_inc(pl_done, 1)

            folded_lo(0)
            folded_lo(1)
            folded_lo(2)
            dve.wait_ge(ch_done, 1)
            nc.vector.tensor_tensor(c_lo[:, :], w2_cols(ps_c), c_hi[:, :].bitcast(F32),
                                    ALU.subtract).then_inc(cl_done, 1)
            dve.wait_ge(brh_done, 1)
            nc.vector.tensor_tensor(br_lo, w2_cols(ps_b)[0:1, :], br_hi.bitcast(F32),
                                    ALU.subtract).then_inc(br_done, 1)
            folded_lo(3)

            def split_experts_lo(q):
                js = slice(q * GC // 4, (q + 1) * GC // 4)
                dve.wait_ge(eh_done, q + 1)
                nc.vector.tensor_tensor(e_lo[:, js, :], exp_raw[:, js, :], e_hi[:, js, :].bitcast(F32),
                                        ALU.subtract).then_inc(el_vector, 1)

            split_experts_lo(2)
            split_experts_lo(3)

            def lora_lo(t, par):
                dve.wait_ge(hh_done, t + 1)
                nc.vector.scalar_tensor_tensor(
                    out=h_stack[:, 2 * R:3 * R].bitcast(F32R), in0=ps_z[par][:, z_lora:z_small],
                    scalar=LORA_SCALE, in1=h_stack[:, 0:R],
                    op0=ALU.mult, op1=ALU.subtract).then_inc(hl_done, 1)

            def route(t, par):
                xt = xn[:, bass.ds(t, 1), :].rearrange("p o n -> p (o n)")
                dve.wait_ge(small_done, t + 1)
                if not (isinstance(t, int) and t == 0):
                    dve.wait_ge(exp_done, t)
                nc.vector.tensor_reduce(neg_max[:, :], small[:, RH:SMALL], AX_X, ALU.max,
                                        negate=True).then_inc(max_done, 1)
                nc.vector.tensor_tensor(xt, ps_z[par][:, z_base:z_base + D], xt, ALU.add).then_inc(acc_done, 1)
                dve.wait_ge(consts, 7)
                dve.wait_ge(exp_done, t + 1)
                nc.vector.max(top8[:, :], probs[:, :]).then_inc(top_done, 1)
                dve.wait_ge(top_done, t + 1)
                nc.vector.tensor_copy(chosen[:, 0:2], top8[:, 0:2]).then_inc(chosen_done, 1)
                nc.vector.tensor_scalar(den0[:, :], prob_sum[:, :], TOPW_EPS, top8[:, 0:1],
                                        ALU.mult, ALU.add).then_inc(den0_done, 1)
                dve.wait_ge(consts, 7)
                dve.wait_ge(chosen_done, t + 1)
                nc.vector.match_replace(rest[:, :], chosen[:, :], probs[:, :], 0.0).then_inc(rest_done, 1)
                dve.wait_ge(den0_done, t + 1)
                nc.vector.tensor_scalar(den[:, :], den0[:, :], top8[:, 1:2], 1.0 / DELTA_SCALE,
                                        ALU.add, ALU.mult).then_inc(den_done, 1)
                dve.wait_ge(rest_done, t + 1)
                nc.vector.tensor_tensor(picked[:, :], probs[:, 0:E], rest[:, 0:E],
                                        ALU.subtract).then_inc(picked_done, 1)
                dve.wait_ge(den_done, t + 1)
                nc.vector.reciprocal(rden[:, :], den[:, :]).then_inc(rden_done, 1)
                dve.wait_ge(picked_done, t + 1)
                dve.wait_ge(rden_done, t + 1)
                if not (isinstance(t, int) and t == 0):
                    dve.wait_ge(pe_gt, 2 * t)
                for half in range(2):
                    es = slice(half * E // 2, (half + 1) * E // 2)
                    nc.vector.scalar_tensor_tensor(
                        out=g[:, half * GN // 2:(half + 1) * GN // 2].rearrange("p (e r) -> p e r", r=RH),
                        in0=small[:, 0:RH].unsqueeze(1).to_broadcast([P, E // 2, RH]), scalar=rden[:, 0:1],
                        in1=picked[:, es].unsqueeze(2).to_broadcast([P, E // 2, RH]),
                        op0=ALU.mult, op1=ALU.mult).then_inc(g_done, 1)

            def g_lo(t, par):
                for half in range(2):
                    dve.wait_ge(gh_done, 2 * t + half + 1)
                    js = slice(half * GC // 2, (half + 1) * GC // 2)
                    nc.vector.tensor_tensor(gt_lo[:, par, js, :].rearrange("p j n -> p (j n)"),
                                            ps_gt[half],
                                            gt_hi[:, par, js, :].rearrange("p j n -> p (j n)").bitcast(F32),
                                            ALU.subtract).then_inc(gl_done, 1)

            def finish(t, par):
                dve.wait_ge(pe_d, t + 1)
                dve.wait_ge(acc_done, t + 1)
                xt = xn[:, bass.ds(t, 1), :].rearrange("p o n -> p (o n)")
                nc.vector.tensor_tensor(xt, ps_d[par], xt, ALU.add).then_inc(out_done, 1)

            dve.wait_ge(in_xn, 16)
            dve.wait_ge(consts, 7)
            for t in range(2):
                lora_lo(t, t)
                route(t, t)
            g_lo(0, 0)
            with dve.Fori(0, NT // 2 - 1) as pair:
                t0 = 2 * pair
                for u in range(2):
                    t = t0 + u
                    lora_lo(t + 2, u)
                    g_lo(t + 1, 1 - u)
                    route(t + 2, u)
                    finish(t, u)
            g_lo(NT - 1, (NT - 1) % 2)
            for t in range(NT - 2, NT):
                finish(t, t % 2)

        @block.tensor
        def _(pe):
            def mm(out_ap, lhs, rhs, first, last):
                return nc.tensor.matmul(out_ap, lhs, rhs, start=first, stop=last)

            def halves(pair, lo_col, border, lhs, rhs, first, last):
                mm(pair[:, lo_col:BANK], lhs, rhs[:, 0:border], first, last)
                n = rhs.shape[-1] - border
                return mm(pair[:, BANK:BANK + n], lhs, rhs[:, border:], first, last)

            pe.wait_ge(warm, 1)
            for _ in range(WARM_UP):
                last = mm(ps_gt[1], zeros[:, 0:P], zeros, True, True)
            last.then_inc(pe_warm, 1)

            def fold_pass(m, k, lhs, rhs, first, last):
                return halves(pairs[m], BANK - W2H, W2H, lhs[:, k, m * P:(m + 1) * P],
                              rhs[:, k, D:], first, last)

            pe.wait_ge(wh_first, 1)
            for k in range(KC - 1):
                pe.wait_ge(wh_done, k + 1)
                for m in range(KC):
                    fold_pass(m, k, w_hi, w_hi, k == 0, False)
                pe.wait_ge(wl_done, k + 1)
                for m in range(KC):
                    fold_pass(m, k, w_hi, w_lo, False, False)
                    fold_pass(m, k, w_lo, w_hi, False, False)

            def fold_last(m):
                fold_pass(m, KC - 1, w_hi, w_hi, False, False)
                fold_pass(m, KC - 1, w_hi, w_lo, False, False)
                fold_pass(m, KC - 1, w_lo, w_hi, False, True).then_inc(pe_p, 1)

            pe.wait_ge(wh_done, KC)
            pe.wait_ge(wl_done, KC)
            fold_last(0)
            fold_last(1)
            fold_last(2)
            pe.wait_ge(lbh_done, 1)
            pe.wait_ge(lbl_done, 1)
            pe.wait_ge(pl_done, 1)
            for k in range(KC):
                for n, (lhs, rhs) in enumerate(((lb_hi, w_hi), (lb_hi, w_lo), (lb_lo, w_hi))):
                    last = halves(ps_c, BANK - W2H, W2H, lhs[:, k, :], rhs[:, k, D:],
                                  k == 0 and n == 0, k == KC - 1 and n == 2)
            last.then_inc(pe_c, 1)
            pe.wait_ge(consts, 7)
            pe.wait_ge(bp_done, 2)
            pe.wait_ge(pl_done, 2)
            halves(ps_b, BANK - W2H, W2H, ones[:, :], bp_hi[:, :], True, False)
            halves(ps_b, BANK - W2H, W2H, ones[:, :], bp_lo[:, :], False, True).then_inc(pe_bias, 1)
            fold_last(3)

            def x_left(t, par):
                pe.wait_ge(x_done, 2 * t + 2)
                if not (isinstance(t, int) and t < 2):
                    pe.wait_ge(acc_done, t - 1)
                elif t == 0:
                    pe.wait_ge(cl_done, 1)
                else:
                    pe.wait_ge(br_done, 1)
                x_side(t, par, ps_z[par][:, z_lora:BANK], slice(0, MVH)).then_inc(pe_left, 1)

            def x_right(t, par):
                x_side(t, par, ps_z[par][:, BANK:BANK + MVH], slice(MVH, MVN)).then_inc(pe_x, 1)

            def x_side(t, par, out_ap, cols):
                for k in range(KC):
                    if isinstance(t, int) and t == 0:
                        pe.wait_ge(pl_done, k + 1)
                    for n, (lhs, rhs) in enumerate(((x_hi, p_hi), (x_hi, p_lo), (x_lo, p_hi))):
                        last = mm(out_ap, lhs[:, par, k, :], rhs[:, k, cols],
                                  k == 0 and n == 0, k == KC - 1 and n == 2)
                return last

            def lora_transpose(t):
                pe.wait_ge(hh_done, t + 1)
                pe.wait_ge(hl_done, t + 1)
                if isinstance(t, int) and t == 0:
                    pe.wait_ge(pl_done, KC)
                elif isinstance(t, int) and t == 1:
                    pe.wait_ge(ht_done, 1)
                else:
                    pe.wait_ge(gl_done, 2 * t - 3)
                nc.tensor.transpose(ps_ht, h_stack[:, :], ident[:, :]).then_inc(pe_ht, 1)

            def lora_product(t, par, pair):
                pe.wait_ge(ht_done, t + 1)
                pe.wait_ge(stacked[par], 48 * (pair + 1))
                rows = c_stack[:, bass.ds(t, 1), :].rearrange("p o n -> p (o n)")
                border = BANK - z_small
                nc.tensor.matmul(ps_z[par][:, z_small:BANK], ht[:, par, :], rows[:, 0:border],
                                 start=False, stop=True, skip_group_check=True)
                nc.tensor.matmul(ps_z[par][:, BANK:BANK + MVH], ht[:, par, :], rows[:, border:],
                                 start=False, stop=True, skip_group_check=True).then_inc(pe_z, 1)

            def g_transpose(t):
                for half in range(2):
                    pe.wait_ge(g_done, 2 * t + half + 1)
                    if half == 0:
                        pe.wait_ge(ht_done, min(t + 2, NT) if isinstance(t, int) else t + 2)
                    elif not (isinstance(t, int) and t == 0):
                        pe.wait_ge(gl_done, 2 * t)
                    for j in range(GC // 2):
                        c = half * GC // 2 + j
                        last = nc.tensor.transpose(ps_gt[half][:, j * P:(j + 1) * P],
                                                   g[:, c * P:(c + 1) * P], ident[:, :])
                    last.then_inc(pe_gt, 1)

            def experts_product(t, par, chunks):
                if chunks[0] == 0:
                    pe.wait_ge(gh_done, 2 * t + 2)
                    pe.wait_ge(gl_done, 2 * t + 2)
                for c in chunks:
                    for n, (lhs, rhs) in enumerate(((gt_hi, e_hi), (gt_hi, e_lo), (gt_lo, e_hi))):
                        last = mm(ps_d[par], lhs[:, par, c, :], rhs[:, c, :],
                                  c == 0 and n == 0, c == GC - 1 and n == 2)
                if chunks[-1] == GC - 1:
                    last.then_inc(pe_d, 1)

            x_left(0, 0)
            x_right(0, 0)
            lora_transpose(0)
            x_left(1, 1)
            pe.wait_ge(stacked_bias, 32)
            lora_product(0, 0, 0)
            x_right(1, 1)
            lora_transpose(1)
            lora_product(1, 1, 0)
            g_transpose(0)
            pe.wait_ge(eh_done, 4)
            pe.wait_ge(el_gpsimd, 2)
            pe.wait_ge(el_vector, 2)

            def iteration(t, par, pair, more, after):
                if more:
                    x_left(t + 2, par)
                    x_right(t + 2, par)
                experts_product(t, par, (0, 1, 2))
                if more:
                    lora_transpose(t + 2)
                if after:
                    g_transpose(t + 1)
                experts_product(t, par, (3, 4, 5))
                if more:
                    lora_product(t + 2, par, pair + 1)
                experts_product(t, par, (6, 7))

            with pe.Fori(0, NT // 2 - 1) as pair:
                t0 = 2 * pair
                for u in range(2):
                    iteration(t0 + u, u, pair, True, True)
            iteration(NT - 2, 0, NT // 2 - 1, False, True)
            iteration(NT - 1, 1, NT // 2 - 1, False, False)


def kernel(x, itok_B_0_23, L0_cond_W, L0_cond_b, L0_cond_lora_As, L0_cond_lora_Bs, L0_ffn_base_w,
           L0_ffn_base_b, L0_ffn_A, L0_ffn_B, L0_ffn_router_w):
    import numpy as np
    import concourse.bacc as bacc
    from concourse.bass_utils import run_bass_kernel_spmd

    c = np.ascontiguousarray
    x = np.asarray(x)
    x_t = c(x.reshape(NT, P, KC, P).transpose(3, 0, 2, 1).reshape(P, NT, KC * P))
    x_n = c(x.transpose(1, 0, 2))
    w2 = np.concatenate([np.asarray(L0_ffn_A).T, np.asarray(L0_ffn_router_w).T,
                         np.asarray(L0_ffn_base_w).T], axis=1)
    w_cat = c(np.concatenate([np.asarray(L0_cond_W), w2], axis=1).reshape(KC, P, D + W2N))
    a = np.asarray(L0_cond_lora_As).reshape(SLOTS, KC, P, R).transpose(0, 2, 1, 3).reshape(SLOTS, P, KC * R)
    b = np.asarray(L0_cond_lora_Bs).reshape(SLOTS, R, KC, P).transpose(0, 3, 2, 1).reshape(SLOTS, P, KC * R)
    tables = c(np.concatenate([a, b], axis=2))
    ex = np.asarray(L0_ffn_B).transpose(0, 2, 1).reshape(GC, P, D)
    arrays = {
        "x_t": x_t, "x_n": x_n, "w_cat": w_cat, "tables": tables,
        "slots": c(np.asarray(itok_B_0_23).reshape(1, NT)),
        "b1": c(np.asarray(L0_cond_b).reshape(KC, P).T), "b2": c(np.asarray(L0_ffn_base_b).reshape(1, D)),
        "experts": c(ex.transpose(1, 0, 2)),
    }
    nc = bacc.Bacc("TRN2", target_bir_lowering=False, num_devices=1)
    aps = [nc.dram_tensor(n, v.shape, mybir.dt.from_np(v.dtype), kind="ExternalInput").ap()
           for n, v in arrays.items()]
    out = nc.dram_tensor("out", (NT, P, D), F32, kind="ExternalOutput").ap()
    adaln_ffn_kernel(nc, *aps, out)
    r = run_bass_kernel_spmd(nc, [arrays], core_ids=[0])
    return r.results[0]["out"]
```

```python
from contextlib import ExitStack

import concourse.bass as bass
from concourse import mybir

F32 = mybir.dt.float32
F32R = mybir.dt.float32r
I32 = mybir.dt.int32
ALU = mybir.AluOpType
ACT = mybir.ActivationFunctionType
AX_X = mybir.AxisListType.X

P = 128
NT = 8
D = 512
KC = D // P
R = 16
RH = 64
E = 16
SMALL = RH + E
W2N = D + SMALL
MVN = R + W2N
W2H = W2N // 2
MVH = MVN // 2
BANK = 512
GN = E * RH
GC = GN // P
SLOTS = 32
AL = 2 * KC * R
LORA_SCALE = 2.0
DELTA_SCALE = 0.5
TOPW_EPS = 1e-6
HR = 3 * R
FOLDS = (2, 1, 0, 3)
W_LEFT, W_RIGHT = slice(0, D // 2), slice(D // 2, D)
W2_LEFT, W2_RIGHT = slice(D, D + W2H), slice(D + W2H, D + W2N)
WARM_UP = 13


def adaln_ffn_kernel(nc, x_t, x_n, w_cat, tables, slots, b1, b2, experts, out):
    with ExitStack() as ctx:
        def sb(name, shape, dt=F32):
            return ctx.enter_context(nc.sbuf_tensor(name, shape, dt))

        def bank(name, shape=(P, D)):
            return ctx.enter_context(nc.psum_tensor(name, list(shape), F32))

        def sem(name):
            return ctx.enter_context(nc.semaphore(name))

        xt_raw = sb("xt_raw", [P, NT, KC * P])
        xn = sb("xn", [P, NT, D])
        w_raw_all = sb("w_raw_all", [P, KC * (D + W2N)])
        w_raw = w_raw_all[:, :].rearrange("p (k n) -> p k n", k=KC)
        lora_raw = sb("lora_raw", [P, NT, AL])
        exp_raw = sb("exp_raw", [P, GC, D])
        slot_row = sb("slot_row", [1, NT], I32)
        b1_col = sb("b1_col", [P, KC])
        b2_row = sb("b2_row", [1, D])
        w_hi_all = sb("w_hi_all", [P, KC * (D + W2N)], F32R)
        w_lo_all = sb("w_lo_all", [P, KC * (D + W2N)], F32R)
        w_hi = w_hi_all[:, :].rearrange("p (k n) -> p k n", k=KC)
        w_lo = w_lo_all[:, :].rearrange("p (k n) -> p k n", k=KC)
        lb_hi = sb("lb_hi", [P, KC, NT * R], F32R)
        lb_lo = sb("lb_lo", [P, KC, NT * R], F32R)
        p_hi = sb("p_hi", [P, KC, MVN], F32R)
        p_lo = sb("p_lo", [P, KC, MVN], F32R)
        c_hi = sb("c_hi", [P, W2N], F32R)
        c_lo = sb("c_lo", [P, W2N], F32R)
        bias_part = sb("bias_part", [P, W2N])
        bp_hi = sb("bp_hi", [P, W2N], F32R)
        bp_lo = sb("bp_lo", [P, W2N], F32R)
        bias = sb("bias", [P, W2N])
        c_stack = sb("c_stack", [HR, NT, W2N], F32R)
        e_hi = sb("e_hi", [P, GC, D], F32R)
        e_lo = sb("e_lo", [P, GC, D], F32R)
        x_hi = sb("x_hi", [P, 2, KC, P], F32R)
        x_lo = sb("x_lo", [P, 2, KC, P], F32R)
        ident = sb("ident", [P, P])
        ones = sb("ones", [P, P], F32R)
        zeros = e_hi[:, 0, 0:2 * P]
        h_stack = sb("h_stack", [P, P])
        ht = sb("ht", [HR, 2, P], F32R)
        small = sb("small", [P, SMALL])
        neg_max = sb("neg_max", [P, 1])
        probs = sb("probs", [P, E + 8])
        prob_sum = sb("prob_sum", [P, 1])
        top8 = sb("top8", [P, 8])
        chosen = sb("chosen", [P, 8])
        rest = sb("rest", [P, E + 8])
        picked = sb("picked", [P, E])
        den0 = sb("den0", [P, 1])
        den = sb("den", [P, 1])
        rden = sb("rden", [P, 1])
        g = w_raw_all[:, 0:GN]
        gt_hi = w_hi_all[:, 0:2 * GC * P].rearrange("p (a j n) -> p a j n", a=2, j=GC)
        gt_lo = w_lo_all[:, 0:2 * GC * P].rearrange("p (a j n) -> p a j n", a=2, j=GC)

        pairs = [bank(f"pair{n}", (P, 2 * BANK)) for n in range(4)]
        ps_c = pairs[2]
        ps_b = pairs[1]
        ps_z = pairs[0:2]
        ps_d = [pairs[2][:, 0:BANK], pairs[2][:, BANK:]]
        ps_gt = [pairs[3][:, 0:BANK], pairs[3][:, BANK:]]
        ps_last = [ps_d[1][:, 0:D // 2], pairs[0][:, 0:D // 2]]
        ps_ht = ps_gt[0][:, 0:P]

        def w2_cols(ps):
            return ps[:, BANK - W2H:BANK + W2H]

        z_lora = BANK - MVH
        z_small = z_lora + R
        z_base = z_small + SMALL

        in_w = [sem(f"in_w{k}") for k in range(KC)]
        in_w2_left = sem("in_w2_left")
        in_w_left = sem("in_w_left")
        in_w2_right = sem("in_w2_right")
        in_slots = sem("in_slots")
        in_lora = sem("in_lora")
        in_b = sem("in_b")
        in_xt = [sem("in_xt_first"), sem("in_xt_next"), sem("in_xt_rest")]
        in_exp = [sem(f"in_exp{q}") for q in range(4)]
        in_xn = [sem("in_xn_first"), sem("in_xn_rest")]
        stacked = [sem("stacked_even"), sem("stacked_odd")]
        stored = sem("stored")
        wh_first = sem("wh_first")
        wh_left = sem("wh_left")
        wh_done = sem("wh_done")
        wl_first = sem("wl_first")
        wl_done = sem("wl_done")
        lbh_done = sem("lbh_done")
        lbl_done = sem("lbl_done")
        pe_p = sem("pe_p")
        ph_done = sem("ph_done")
        pl_done = sem("pl_done")
        pe_c = sem("pe_c")
        ch_done = sem("ch_done")
        cl_done = sem("cl_done")
        bias_step = sem("bias_step")
        bph_done = sem("bph_done")
        bpl_done = sem("bpl_done")
        pe_bias = sem("pe_bias")
        bias_done = sem("bias_done")
        eh_done = sem("eh_done")
        el_done = sem("el_done")
        warm = sem("warm")
        pe_warm = sem("pe_warm")
        consts = sem("consts")
        xh_done = sem("xh_done")
        lah_done = sem("lah_done")
        x_done = sem("x_done")
        biased = sem("biased")
        pe_left = sem("pe_left")
        pe_x = sem("pe_x")
        hh_done = sem("hh_done")
        hl_done = sem("hl_done")
        pe_ht = sem("pe_ht")
        ht_done = sem("ht_done")
        pe_z = sem("pe_z")
        small_done = sem("small_done")
        max_done = sem("max_done")
        exp_done = sem("exp_done")
        top_done = sem("top_done")
        chosen_done = sem("chosen_done")
        rest_done = sem("rest_done")
        picked_done = sem("picked_done")
        den0_done = sem("den0_done")
        den_done = sem("den_done")
        rden_done = sem("rden_done")
        g_done = sem("g_done")
        acc_done = sem("acc_done")
        pe_gt = sem("pe_gt")
        gh_done = sem("gh_done")
        gl_done = sem("gl_done")
        pe_d = sem("pe_d")
        out_done = sem("out_done")

        block = ctx.enter_context(nc.Block())

        @block.sync
        def _(sp):
            def load_w(k):
                sp.dma_start(w_raw[:, k, :], w_cat[k]).then_inc(in_w[k], 16)

            def load_experts(q):
                js = slice(q * GC // 4, (q + 1) * GC // 4)
                sp.dma_start(exp_raw[:, js, :], experts[:, js, :]).then_inc(in_exp[q], 16)

            for cols, landed in ((W2_LEFT, in_w2_left), (W_LEFT, in_w_left), (W2_RIGHT, in_w2_right),
                                 (W_RIGHT, in_w[0])):
                sp.dma_start(w_raw[:, 0, cols], w_cat[0, :, cols]).then_inc(landed, 16)
            sp.dma_start(slot_row[:, :], slots).then_inc(in_slots, 16)
            load_w(1)
            sp.dma_start(b1_col[:, :], b1).then_inc(in_b, 16)
            load_w(2)
            sp.dma_start(b2_row[:, :], b2).then_inc(in_b, 16)
            load_w(3)
            sp.dma_start(xt_raw[:, 0:2, :], x_t[:, 0:2, :]).then_inc(in_xt[0], 16)
            sp.wait_ge(in_slots, 16)
            for t in range(NT):
                slot = sp.value_load(slot_row[0:1, t:t + 1], min_val=0, max_val=SLOTS - 1)
                src = tables[bass.ds(slot, 1), :, :].rearrange("o p n -> p (o n)")
                sp.dma_start(lora_raw[:, t, :], src).then_inc(in_lora, 16)
            for q in range(4):
                load_experts(q)
            sp.dma_start(xn[:, 0:2, :], x_n[:, 0:2, :]).then_inc(in_xn[0], 16)
            sp.dma_start(xt_raw[:, 2:4, :], x_t[:, 2:4, :]).then_inc(in_xt[1], 16)

            def stack(t):
                if t >= 2:
                    sp.wait_ge(stacked[t % 2], 48 * (t // 2))
                for n, part in ((0, c_hi), (2, c_hi), (1, c_lo)):
                    if t == 0 and n == 1:
                        sp.wait_ge(cl_done, 1)
                    sp.dma_start(c_stack[n * R:(n + 1) * R, t, :].bitcast(F32),
                                 part[t * R:(t + 1) * R, :].bitcast(F32)).then_inc(stacked[t % 2], 16)

            sp.wait_ge(ch_done, 1)
            stack(0)
            sp.dma_start(xt_raw[:, 4:NT, :], x_t[:, 4:NT, :]).then_inc(in_xt[2], 16)
            stack(1)
            stack(2)
            sp.dma_start(xn[:, 2:NT, :], x_n[:, 2:NT, :]).then_inc(in_xn[1], 16)
            for t in range(3, NT):
                stack(t)
            with sp.Fori(0, NT - 1) as t:
                sp.wait_ge(out_done, t + 1)
                dst = out[bass.ds(t, 1), :, :].rearrange("o p n -> p (o n)")
                src = xn[:, bass.ds(t, 1), :].rearrange("p o n -> p (o n)")
                sp.dma_start(dst, src).then_inc(stored, 16)
            for half in range(2):
                cols = slice(half * D // 2, (half + 1) * D // 2)
                sp.wait_ge(out_done, NT + half)
                sp.dma_start(out[NT - 1, :, cols], xn[:, NT - 1, cols]).then_inc(stored, 16)
            sp.wait_ge(stored, 16 * (NT + 1))

        @block.gpsimd
        def _(pool):
            pool.memset(ident[:, :], 0.0).then_inc(consts, 1)
            pool.wait_ge(consts, 1)
            pool.affine_select(out=ident[:, :], in_=ident[:, :], compare_op=ALU.not_equal, fill=1.0,
                               base=0, pattern=[[-1, P]], channel_multiplier=1).then_inc(consts, 1)
            pool.memset(ones[:, :].bitcast(F32), 1.0).then_inc(consts, 1)
            pool.memset(probs[:, E:E + 8], -1.0).then_inc(consts, 1)
            pool.memset(chosen[:, 2:8], -1.0).then_inc(consts, 1)
            pool.memset(h_stack[:, HR:P], 0.0).then_inc(consts, 1)

            def x_lo_part(t, par):
                xt = xt_raw[:, bass.ds(t, 1), :].rearrange("p o n -> p (o n)")
                pool.wait_ge(xh_done, t + 1)
                pool.tensor_tensor(x_lo[:, par].rearrange("p k n -> p (k n)"), xt,
                                   x_hi[:, par].rearrange("p k n -> p (k n)").bitcast(F32),
                                   ALU.subtract).then_inc(x_done, 1)

            def lora_a_parts(t):
                la = lora_raw[:, bass.ds(t, 1), 0:KC * R].rearrange("p o (k r) -> p (o k) r", k=KC)
                pool.wait_ge(in_lora, 16 * NT)
                if not (isinstance(t, int) and t == 0):
                    pool.wait_ge(pe_left, t)
                pool.tensor_copy(p_hi[:, :, 0:R], la).then_inc(lah_done, 1)
                pool.wait_ge(in_lora, 16 * NT)
                pool.wait_ge(lah_done, t + 1)
                pool.tensor_tensor(p_lo[:, :, 0:R], la, p_hi[:, :, 0:R].bitcast(F32),
                                   ALU.subtract).then_inc(x_done, 1)

            def add_bias(t):
                xt = xn[:, bass.ds(t, 1), :].rearrange("p o n -> p (o n)")
                pool.wait_ge(bias_done, 1)
                pool.tensor_tensor(xt, xt, bias[:, SMALL:], ALU.add).then_inc(biased, 1)

            x_lo_part(0, 0)
            lora_a_parts(0)
            x_lo_part(1, 1)
            pool.wait_ge(in_xn[0], 16)
            lora_a_parts(1)
            add_bias(0)
            x_lo_part(2, 0)
            lora_a_parts(2)
            add_bias(1)
            with pool.Fori(0, (NT - 4) // 2) as pair:
                t0 = 2 * pair
                for u in range(2):
                    x_lo_part(t0 + 3 + u, 1 - u)
                    lora_a_parts(t0 + 3 + u)
                    pool.wait_ge(in_xn[1], 16)
                    add_bias(t0 + 2 + u)
            x_lo_part(NT - 1, 1)
            lora_a_parts(NT - 1)
            for t in (NT - 2, NT - 1):
                add_bias(t)

        @block.scalar
        def _(act):
            act.wait_ge(in_w_left, 16)
            nc.scalar.activation(w_hi[:, 0, W_LEFT], w_raw[:, 0, W_LEFT], ACT.Copy).then_inc(wh_left, 1)
            act.wait_ge(in_w[0], 16)
            nc.scalar.activation(w_hi[:, 0, W_RIGHT], w_raw[:, 0, W_RIGHT], ACT.Copy).then_inc(wh_done, 1)
            for k in range(1, KC):
                act.wait_ge(in_w[k], 16)
                nc.scalar.activation(w_hi[:, k, :], w_raw[:, k, :], ACT.Copy).then_inc(wh_done, 1)

            def x_hi_part(t, par):
                xt = xt_raw[:, bass.ds(t, 1), :].rearrange("p o n -> p (o n)")
                if not (isinstance(t, int) and t < 2):
                    act.wait_ge(pe_x, t - 1)
                nc.scalar.activation(x_hi[:, par].rearrange("p k n -> p (k n)"), xt,
                                     ACT.Copy).then_inc(xh_done, 1)

            def split_experts(q):
                js = slice(q * GC // 4, (q + 1) * GC // 4)
                act.wait_ge(in_exp[q], 16)
                nc.scalar.activation(e_hi[:, js, :], exp_raw[:, js, :], ACT.Copy).then_inc(eh_done, 1)

            def folded_hi(n):
                act.wait_ge(pe_p, n + 1)
                nc.scalar.activation(p_hi[:, FOLDS[n], R:], w2_cols(pairs[FOLDS[n]]),
                                     ACT.Copy).then_inc(ph_done, 1)

            act.wait_ge(in_xt[0], 16)
            x_hi_part(0, 0)
            x_hi_part(1, 1)
            folded_hi(0)
            act.wait_ge(in_lora, 16 * NT)
            nc.scalar.activation(lb_hi[:, :, :].rearrange("p k (t r) -> p t k r", t=NT),
                                 lora_raw[:, :, KC * R:AL].rearrange("p t (k r) -> p t k r", k=KC),
                                 ACT.Copy).then_inc(lbh_done, 1)
            folded_hi(1)
            act.wait_ge(bias_step, KC + 1)
            nc.scalar.activation(bp_hi[:, :], bias_part[:, :], ACT.Copy).then_inc(bph_done, 1)
            folded_hi(2)
            folded_hi(3)
            act.wait_ge(pe_warm, 1)
            for q in range(3):
                split_experts(q)
            act.wait_ge(pe_c, 1)
            nc.scalar.activation(c_hi[:, :], w2_cols(ps_c), ACT.Copy).then_inc(ch_done, 1)
            act.wait_ge(pe_bias, 1)
            nc.scalar.activation(bias[:, :], w2_cols(ps_b), ACT.Copy).then_inc(bias_done, 1)

            def lora_hi(t, par):
                act.wait_ge(pe_left, t + 1)
                if not (isinstance(t, int) and t == 0):
                    act.wait_ge(pe_ht, t)
                src = ps_z[par][:, z_lora:z_small].unsqueeze(1).to_broadcast([P, 2, R])
                dst = h_stack[:, 0:2 * R].rearrange("p (a r) -> p a r", a=2).bitcast(F32R)
                nc.scalar.activation(dst, src, ACT.Copy, scale=LORA_SCALE).then_inc(hh_done, 1)

            def lora_t(t, par):
                act.wait_ge(pe_ht, t + 1)
                if not (isinstance(t, int) and t < 2):
                    act.wait_ge(pe_z, t - 1)
                nc.scalar.activation(ht[:, par, :], ps_ht[0:HR, :], ACT.Copy).then_inc(ht_done, 1)

            def exps(t):
                act.wait_ge(small_done, t + 1)
                act.wait_ge(max_done, t + 1)
                if not (isinstance(t, int) and t == 0):
                    act.wait_ge(picked_done, t)
                    act.wait_ge(den0_done, t)
                else:
                    act.wait_ge(consts, 6)
                nc.scalar.activation(probs[:, 0:E], small[:, RH:SMALL], ACT.Exp, bias=neg_max[:, 0:1],
                                     accum_out=prob_sum[:, 0:1]).then_inc(exp_done, 1)

            def g_hi(t, par):
                for half in range(2):
                    act.wait_ge(pe_gt, 2 * t + half + 1)
                    dst = gt_hi[:, par, half * GC // 2:(half + 1) * GC // 2, :]
                    nc.scalar.activation(dst.rearrange("p j n -> p (j n)"), ps_gt[half],
                                         ACT.Copy).then_inc(gh_done, 1)

            def iteration(t, par, ahead):
                if ahead:
                    x_hi_part(t + 3, 1 - par)
                lora_t(t + 2, par)
                g_hi(t + 1, 1 - par)
                exps(t + 2)
                if ahead:
                    lora_hi(t + 3, 1 - par)

            lora_hi(0, 0)
            split_experts(3)
            act.wait_ge(in_xt[1], 16)
            x_hi_part(2, 0)
            lora_t(0, 0)
            lora_hi(1, 1)
            exps(0)
            lora_t(1, 1)
            g_hi(0, 0)
            exps(1)
            lora_hi(2, 0)
            act.wait_ge(in_xt[2], 16)
            with act.Fori(0, (NT - 4) // 2) as pair:
                t0 = 2 * pair
                for u in range(2):
                    iteration(t0 + u, u, True)
            iteration(NT - 4, 0, True)
            iteration(NT - 3, 1, False)
            g_hi(NT - 1, (NT - 1) % 2)

        @block.vector
        def _(dve):
            nc.vector.memset(zeros.bitcast(F32), 0.0).then_inc(warm, 1)
            dve.wait_ge(in_w2_left, 16)
            nc.vector.tensor_copy(w_hi[:, 0, W2_LEFT], w_raw[:, 0, W2_LEFT]).then_inc(wh_first, 1)
            dve.wait_ge(in_w2_right, 16)
            nc.vector.tensor_copy(w_hi[:, 0, W2_RIGHT], w_raw[:, 0, W2_RIGHT]).then_inc(wh_first, 1)
            dve.wait_ge(wh_first, 2)
            nc.vector.tensor_tensor(w_lo[:, 0, D:], w_raw[:, 0, D:], w_hi[:, 0, D:].bitcast(F32),
                                    ALU.subtract).then_inc(wl_first, 1)
            dve.wait_ge(wh_left, 1)
            dve.wait_ge(wh_done, 1)
            nc.vector.tensor_tensor(w_lo[:, 0, 0:D], w_raw[:, 0, 0:D], w_hi[:, 0, 0:D].bitcast(F32),
                                    ALU.subtract).then_inc(wl_done, 1)
            for k in range(1, KC):
                dve.wait_ge(wh_done, k + 1)
                nc.vector.tensor_tensor(w_lo[:, k, :], w_raw[:, k, :], w_hi[:, k, :].bitcast(F32),
                                        ALU.subtract).then_inc(wl_done, 1)
            dve.wait_ge(in_b, 32)
            nc.vector.tensor_scalar(bias_part[:, :], w_raw[:, 0, D:], b1_col[:, 0:1], None,
                                    ALU.mult).then_inc(bias_step, 1)
            for k in range(1, KC):
                dve.wait_ge(bias_step, k)
                nc.vector.scalar_tensor_tensor(out=bias_part[:, :], in0=w_raw[:, k, D:],
                                               scalar=b1_col[:, k:k + 1], in1=bias_part[:, :],
                                               op0=ALU.mult, op1=ALU.add).then_inc(bias_step, 1)
            dve.wait_ge(bias_step, KC)
            nc.vector.tensor_tensor(bias_part[0:1, SMALL:], bias_part[0:1, SMALL:], b2_row[0:1, :],
                                    ALU.add).then_inc(bias_step, 1)

            def folded_lo(n):
                dve.wait_ge(ph_done, n + 1)
                m = FOLDS[n]
                nc.vector.tensor_tensor(p_lo[:, m, R:], w2_cols(pairs[m]), p_hi[:, m, R:].bitcast(F32),
                                        ALU.subtract).then_inc(pl_done, 1)

            def split_experts_lo(q):
                js = slice(q * GC // 4, (q + 1) * GC // 4)
                dve.wait_ge(eh_done, q + 1)
                nc.vector.tensor_tensor(e_lo[:, js, :], exp_raw[:, js, :], e_hi[:, js, :].bitcast(F32),
                                        ALU.subtract).then_inc(el_done, 1)

            folded_lo(0)
            dve.wait_ge(lbh_done, 1)
            nc.vector.tensor_tensor(lb_lo[:, :, :].rearrange("p k (t r) -> p t k r", t=NT),
                                    lora_raw[:, :, KC * R:AL].rearrange("p t (k r) -> p t k r", k=KC),
                                    lb_hi[:, :, :].rearrange("p k (t r) -> p t k r", t=NT).bitcast(F32),
                                    ALU.subtract).then_inc(lbl_done, 1)
            folded_lo(1)
            folded_lo(2)
            dve.wait_ge(bph_done, 1)
            nc.vector.tensor_tensor(bp_lo[:, :], bias_part[:, :], bp_hi[:, :].bitcast(F32),
                                    ALU.subtract).then_inc(bpl_done, 1)
            folded_lo(3)
            split_experts_lo(0)
            split_experts_lo(1)
            dve.wait_ge(ch_done, 1)
            nc.vector.tensor_tensor(c_lo[:, :], w2_cols(ps_c), c_hi[:, :].bitcast(F32),
                                    ALU.subtract).then_inc(cl_done, 1)

            def lora_lo(t, par):
                dve.wait_ge(hh_done, t + 1)
                nc.vector.scalar_tensor_tensor(
                    out=h_stack[:, 2 * R:3 * R].bitcast(F32R), in0=ps_z[par][:, z_lora:z_small],
                    scalar=LORA_SCALE, in1=h_stack[:, 0:R],
                    op0=ALU.mult, op1=ALU.subtract).then_inc(hl_done, 1)

            def read_z(t, par):
                xt = xn[:, bass.ds(t, 1), :].rearrange("p o n -> p (o n)")
                dve.wait_ge(pe_z, t + 1)
                if not (isinstance(t, int) and t == 0):
                    dve.wait_ge(g_done, 2 * t)
                    dve.wait_ge(exp_done, t)
                else:
                    dve.wait_ge(bias_done, 1)
                nc.vector.tensor_tensor(small[:, :], ps_z[par][:, z_small:z_base], bias[:, 0:SMALL],
                                        ALU.add).then_inc(small_done, 1)
                dve.wait_ge(small_done, t + 1)
                nc.vector.tensor_reduce(neg_max[:, :], small[:, RH:SMALL], AX_X, ALU.max,
                                        negate=True).then_inc(max_done, 1)
                dve.wait_ge(biased, t + 1)
                nc.vector.tensor_tensor(xt, ps_z[par][:, z_base:z_base + D], xt, ALU.add).then_inc(acc_done, 1)

            def route(t):
                dve.wait_ge(consts, 6)
                dve.wait_ge(exp_done, t + 1)
                nc.vector.max(top8[:, :], probs[:, :]).then_inc(top_done, 1)
                dve.wait_ge(top_done, t + 1)
                nc.vector.tensor_copy(chosen[:, 0:2], top8[:, 0:2]).then_inc(chosen_done, 1)
                nc.vector.tensor_scalar(den0[:, :], prob_sum[:, :], TOPW_EPS, top8[:, 0:1],
                                        ALU.mult, ALU.add).then_inc(den0_done, 1)
                dve.wait_ge(consts, 6)
                dve.wait_ge(chosen_done, t + 1)
                nc.vector.match_replace(rest[:, :], chosen[:, :], probs[:, :], 0.0).then_inc(rest_done, 1)
                dve.wait_ge(den0_done, t + 1)
                nc.vector.tensor_scalar(den[:, :], den0[:, :], top8[:, 1:2], 1.0 / DELTA_SCALE,
                                        ALU.add, ALU.mult).then_inc(den_done, 1)
                dve.wait_ge(rest_done, t + 1)
                nc.vector.tensor_tensor(picked[:, :], probs[:, 0:E], rest[:, 0:E],
                                        ALU.subtract).then_inc(picked_done, 1)
                dve.wait_ge(den_done, t + 1)
                nc.vector.reciprocal(rden[:, :], den[:, :]).then_inc(rden_done, 1)
                dve.wait_ge(picked_done, t + 1)
                dve.wait_ge(rden_done, t + 1)
                if not (isinstance(t, int) and t == 0):
                    dve.wait_ge(pe_gt, 2 * t)
                for half in range(2):
                    es = slice(half * E // 2, (half + 1) * E // 2)
                    nc.vector.scalar_tensor_tensor(
                        out=g[:, half * GN // 2:(half + 1) * GN // 2].rearrange("p (e r) -> p e r", r=RH),
                        in0=small[:, 0:RH].unsqueeze(1).to_broadcast([P, E // 2, RH]), scalar=rden[:, 0:1],
                        in1=picked[:, es].unsqueeze(2).to_broadcast([P, E // 2, RH]),
                        op0=ALU.mult, op1=ALU.mult).then_inc(g_done, 1)

            def g_lo(t, par):
                for half in range(2):
                    dve.wait_ge(gh_done, 2 * t + half + 1)
                    js = slice(half * GC // 2, (half + 1) * GC // 2)
                    nc.vector.tensor_tensor(gt_lo[:, par, js, :].rearrange("p j n -> p (j n)"),
                                            ps_gt[half],
                                            gt_hi[:, par, js, :].rearrange("p j n -> p (j n)").bitcast(F32),
                                            ALU.subtract).then_inc(gl_done, 1)

            def finish(t, par):
                dve.wait_ge(pe_d, t + 1)
                dve.wait_ge(acc_done, t + 1)
                xt = xn[:, bass.ds(t, 1), :].rearrange("p o n -> p (o n)")
                nc.vector.tensor_tensor(xt, ps_d[par], xt, ALU.add).then_inc(out_done, 1)

            lora_lo(0, 0)
            split_experts_lo(2)
            split_experts_lo(3)
            read_z(0, 0)
            lora_lo(1, 1)
            route(0)
            read_z(1, 1)
            g_lo(0, 0)
            lora_lo(2, 0)
            route(1)

            def iteration(t, par, ahead):
                g_lo(t + 1, 1 - par)
                read_z(t + 2, par)
                route(t + 2)
                if ahead:
                    lora_lo(t + 3, 1 - par)
                finish(t, par)

            with dve.Fori(0, (NT - 4) // 2) as pair:
                t0 = 2 * pair
                for u in range(2):
                    iteration(t0 + u, u, True)
            iteration(NT - 4, 0, True)
            iteration(NT - 3, 1, False)
            g_lo(NT - 1, (NT - 1) % 2)
            finish(NT - 2, (NT - 2) % 2)
            for half in range(2):
                cols = slice(half * D // 2, (half + 1) * D // 2)
                dve.wait_ge(pe_d, NT + half)
                dve.wait_ge(acc_done, NT)
                nc.vector.tensor_tensor(xn[:, NT - 1, cols], ps_last[half], xn[:, NT - 1, cols],
                                        ALU.add).then_inc(out_done, 1)

        @block.tensor
        def _(pe):
            def mm(out_ap, lhs, rhs, first, last):
                return nc.tensor.matmul(out_ap, lhs, rhs, start=first, stop=last)

            def halves(pair, lo_col, border, lhs, rhs, first, last):
                mm(pair[:, lo_col:BANK], lhs, rhs[:, 0:border], first, last)
                n = rhs.shape[-1] - border
                return mm(pair[:, BANK:BANK + n], lhs, rhs[:, border:], first, last)

            pe.wait_ge(warm, 1)
            for _ in range(WARM_UP):
                last = mm(ps_gt[1][:, 0:2 * P], zeros[:, 0:P], zeros, True, True)
            last.then_inc(pe_warm, 1)

            def fold_pass(m, k, lhs, rhs, first, last):
                return halves(pairs[m], BANK - W2H, W2H, lhs[:, k, m * P:(m + 1) * P],
                              rhs[:, k, D:], first, last)

            def fold_first(m, out_cols, cols):
                mm(pairs[m][:, out_cols], w_hi[:, 0, m * P:(m + 1) * P], w_hi[:, 0, cols], True, False)

            pe.wait_ge(wh_first, 1)
            pe.wait_ge(wh_left, 1)
            fold_first(0, slice(BANK - W2H, BANK), W2_LEFT)
            fold_first(1, slice(BANK - W2H, BANK), W2_LEFT)
            pe.wait_ge(wh_first, 2)
            fold_first(0, slice(BANK, BANK + W2H), W2_RIGHT)
            fold_first(1, slice(BANK, BANK + W2H), W2_RIGHT)
            pe.wait_ge(wh_done, 1)
            for m in range(KC // 2, KC):
                fold_pass(m, 0, w_hi, w_hi, True, False)
            pe.wait_ge(wl_first, 1)
            for m in range(KC):
                fold_pass(m, 0, w_hi, w_lo, False, False)
            pe.wait_ge(wl_done, 1)
            for m in range(KC):
                fold_pass(m, 0, w_lo, w_hi, False, False)
            for k in range(1, KC - 1):
                pe.wait_ge(wh_done, k + 1)
                for m in range(KC):
                    fold_pass(m, k, w_hi, w_hi, False, False)
                pe.wait_ge(wl_done, k + 1)
                for m in range(KC):
                    fold_pass(m, k, w_hi, w_lo, False, False)
                    fold_pass(m, k, w_lo, w_hi, False, False)

            def fold_last(m):
                fold_pass(m, KC - 1, w_hi, w_hi, False, False)
                fold_pass(m, KC - 1, w_hi, w_lo, False, False)
                fold_pass(m, KC - 1, w_lo, w_hi, False, True).then_inc(pe_p, 1)

            pe.wait_ge(wh_done, KC)
            pe.wait_ge(wl_done, KC)
            for m in FOLDS:
                fold_last(m)
            pe.wait_ge(lbh_done, 1)
            pe.wait_ge(lbl_done, 1)
            pe.wait_ge(pl_done, 1)
            for k in range(KC):
                for n, (lhs, rhs) in enumerate(((lb_hi, w_hi), (lb_hi, w_lo), (lb_lo, w_hi))):
                    last = halves(ps_c, BANK - W2H, W2H, lhs[:, k, :], rhs[:, k, D:],
                                  k == 0 and n == 0, k == KC - 1 and n == 2)
            last.then_inc(pe_c, 1)
            pe.wait_ge(consts, 6)
            pe.wait_ge(bph_done, 1)
            pe.wait_ge(bpl_done, 1)
            pe.wait_ge(pl_done, 2)
            halves(ps_b, BANK - W2H, W2H, ones[:, :], bp_hi[:, :], True, False)
            halves(ps_b, BANK - W2H, W2H, ones[:, :], bp_lo[:, :], False, True).then_inc(pe_bias, 1)

            def x_left(t, par):
                pe.wait_ge(x_done, 2 * t + 2)
                if not (isinstance(t, int) and t < 2):
                    pe.wait_ge(acc_done, t - 1)
                elif t == 1:
                    pe.wait_ge(bias_done, 1)
                x_side(t, par, ps_z[par][:, z_lora:BANK], slice(0, MVH)).then_inc(pe_left, 1)

            def x_right(t, par):
                x_side(t, par, ps_z[par][:, BANK:BANK + MVH], slice(MVH, MVN)).then_inc(pe_x, 1)

            def x_side(t, par, out_ap, cols):
                for k in range(KC):
                    if isinstance(t, int) and t == 0 and k == 0:
                        pe.wait_ge(pl_done, KC)
                    for n, (lhs, rhs) in enumerate(((x_hi, p_hi), (x_hi, p_lo), (x_lo, p_hi))):
                        last = mm(out_ap, lhs[:, par, k, :], rhs[:, k, cols],
                                  k == 0 and n == 0, k == KC - 1 and n == 2)
                return last

            def lora_transpose(t):
                pe.wait_ge(hh_done, t + 1)
                pe.wait_ge(hl_done, t + 1)
                if isinstance(t, int) and t == 0:
                    pe.wait_ge(pl_done, KC)
                elif isinstance(t, int) and t == 1:
                    pe.wait_ge(ht_done, 1)
                else:
                    pe.wait_ge(gl_done, 2 * t - 3)
                nc.tensor.transpose(ps_ht, h_stack[:, :], ident[:, :]).then_inc(pe_ht, 1)

            def lora_product(t, par, pair):
                pe.wait_ge(ht_done, t + 1)
                pe.wait_ge(stacked[par], 48 * (pair + 1))
                rows = c_stack[:, bass.ds(t, 1), :].rearrange("p o n -> p (o n)")
                border = BANK - z_small
                nc.tensor.matmul(ps_z[par][:, z_small:BANK], ht[:, par, :], rows[:, 0:border],
                                 start=False, stop=True, skip_group_check=True)
                nc.tensor.matmul(ps_z[par][:, BANK:BANK + MVH], ht[:, par, :], rows[:, border:],
                                 start=False, stop=True, skip_group_check=True).then_inc(pe_z, 1)

            def g_transpose(t):
                for half in range(2):
                    pe.wait_ge(g_done, 2 * t + half + 1)
                    if half == 0:
                        pe.wait_ge(ht_done, min(t + 2, NT) if isinstance(t, int) else t + 2)
                    elif not (isinstance(t, int) and t == 0):
                        pe.wait_ge(gl_done, 2 * t)
                    for j in range(GC // 2):
                        c = half * GC // 2 + j
                        last = nc.tensor.transpose(ps_gt[half][:, j * P:(j + 1) * P],
                                                   g[:, c * P:(c + 1) * P], ident[:, :])
                    last.then_inc(pe_gt, 1)

            def experts_product(t, par, chunks, out_ap, cols):
                for c in chunks:
                    if c in (0, GC // 2):
                        pe.wait_ge(gh_done, 2 * t + (1 if c == 0 else 2))
                        pe.wait_ge(gl_done, 2 * t + (1 if c == 0 else 2))
                    for n, (lhs, rhs) in enumerate(((gt_hi, e_hi), (gt_hi, e_lo), (gt_lo, e_hi))):
                        last = mm(out_ap, lhs[:, par, c, :], rhs[:, c, cols],
                                  c == 0 and n == 0, c == GC - 1 and n == 2)
                if chunks[-1] == GC - 1:
                    last.then_inc(pe_d, 1)

            def iteration(t, par, pair, more, ahead):
                def experts_part(*chunks):
                    experts_product(t, par, chunks, ps_d[par], slice(0, D))

                if more:
                    x_right(t + 2, par)
                experts_part(0)
                if more:
                    lora_transpose(t + 2)
                experts_part(1, 2, 3)
                g_transpose(t + 1)
                experts_part(4, 5)
                if more:
                    lora_product(t + 2, par, pair + 1)
                experts_part(6)
                if ahead:
                    x_left(t + 3, 1 - par)
                experts_part(7)

            x_left(0, 0)
            x_right(0, 0)
            lora_transpose(0)
            x_left(1, 1)
            lora_product(0, 0, 0)
            x_right(1, 1)
            lora_transpose(1)
            x_left(2, 0)
            lora_product(1, 1, 0)
            g_transpose(0)
            pe.wait_ge(eh_done, 4)
            pe.wait_ge(el_done, 4)
            with pe.Fori(0, (NT - 4) // 2) as pair:
                t0 = 2 * pair
                for u in range(2):
                    iteration(t0 + u, u, pair, True, True)
            iteration(NT - 4, 0, NT // 2 - 2, True, True)
            iteration(NT - 3, 1, NT // 2 - 2, True, False)
            iteration(NT - 2, 0, NT // 2 - 1, False, False)
            pe.wait_ge(acc_done, NT - 1)
            for half in range(2):
                experts_product(NT - 1, 1, range(GC), ps_last[half],
                                slice(half * D // 2, (half + 1) * D // 2))


def kernel(x, itok_B_0_23, L0_cond_W, L0_cond_b, L0_cond_lora_As, L0_cond_lora_Bs, L0_ffn_base_w,
           L0_ffn_base_b, L0_ffn_A, L0_ffn_B, L0_ffn_router_w):
    import numpy as np
    import concourse.bacc as bacc
    from concourse.bass_utils import run_bass_kernel_spmd

    c = np.ascontiguousarray
    x = np.asarray(x)
    x_t = c(x.reshape(NT, P, KC, P).transpose(3, 0, 2, 1).reshape(P, NT, KC * P))
    x_n = c(x.transpose(1, 0, 2))
    w2 = np.concatenate([np.asarray(L0_ffn_A).T, np.asarray(L0_ffn_router_w).T,
                         np.asarray(L0_ffn_base_w).T], axis=1)
    w_cat = c(np.concatenate([np.asarray(L0_cond_W), w2], axis=1).reshape(KC, P, D + W2N))
    a = np.asarray(L0_cond_lora_As).reshape(SLOTS, KC, P, R).transpose(0, 2, 1, 3).reshape(SLOTS, P, KC * R)
    b = np.asarray(L0_cond_lora_Bs).reshape(SLOTS, R, KC, P).transpose(0, 3, 2, 1).reshape(SLOTS, P, KC * R)
    tables = c(np.concatenate([a, b], axis=2))
    ex = np.asarray(L0_ffn_B).transpose(0, 2, 1).reshape(GC, P, D)
    arrays = {
        "x_t": x_t, "x_n": x_n, "w_cat": w_cat, "tables": tables,
        "slots": c(np.asarray(itok_B_0_23).reshape(1, NT)),
        "b1": c(np.asarray(L0_cond_b).reshape(KC, P).T), "b2": c(np.asarray(L0_ffn_base_b).reshape(1, D)),
        "experts": c(ex.transpose(1, 0, 2)),
    }
    nc = bacc.Bacc("TRN2", target_bir_lowering=False, num_devices=1)
    aps = [nc.dram_tensor(n, v.shape, mybir.dt.from_np(v.dtype), kind="ExternalInput").ap()
           for n, v in arrays.items()]
    out = nc.dram_tensor("out", (NT, P, D), F32, kind="ExternalOutput").ap()
    adaln_ffn_kernel(nc, *aps, out)
    r = run_bass_kernel_spmd(nc, [arrays], core_ids=[0])
    return r.results[0]["out"]
```
